# Optimizing a Trainium2 kernel written in Bass

```python
import numpy as np
import jax
import jax.numpy as jnp

def _softmax(x, axis=-1):
    return jax.nn.softmax(x, axis=axis)

def _gelu(x):
    return jax.nn.gelu(x, approximate=True)

def _silu(x):
    return jax.nn.silu(x)

def _sigmoid(x):
    return jax.nn.sigmoid(x)

def _layernorm(x, axis=-1, eps=1e-05):
    m = jnp.mean(x, axis=axis, keepdims=True)
    v = jnp.var(x, axis=axis, keepdims=True)
    return (x - m) / jnp.sqrt(v + eps)

def _scatter_add(tgt, idx, src, axis=0):
    return tgt.at[idx].add(src)

def _segment_sum(src, seg, n):
    return jax.ops.segment_sum(src, seg, n)
kernel_name = 'mk_conv_preact_d2_conv_nchw384_r2_e16f35'

def setup_inputs(seed: int=0):
    np.random.seed(seed)
    _w = jnp.asarray

    def _rec_inputs():
        import jax
        import jax.numpy as jnp
        _gk = jax.random.key(seed)
        x = -0.0001476 + 0.9999 * jax.random.normal(jax.random.fold_in(_gk, 1), (32, 192, 56, 56), jnp.float32)
        return x
    x = _rec_inputs()

    def _L0_conv_setup():
        import jax, jax.numpy as jnp
        import numpy as np
        WS, NH = (7, 12)
        DIM, B, H, W = (192, 32, 56, 56)

        def _rel_index(ws):
            coords = np.stack(np.meshgrid(np.arange(ws), np.arange(ws), indexing='ij')).reshape(2, -1)
            rel = (coords[:, :, None] - coords[:, None, :]).transpose(1, 2, 0)
            rel[..., 0] += ws - 1
            rel[..., 1] += ws - 1
            rel[..., 0] *= 2 * ws - 1
            return jnp.asarray(rel.sum(-1), dtype=jnp.int32)
        key = jax.random.key(seed)
        k1, k2, k3, k4, k5 = jax.random.split(key, 5)
        x = jax.random.normal(k1, (B, DIM, H, W), dtype=jnp.float32)
        w_qkv = jax.random.normal(k2, (3 * DIM, DIM), dtype=jnp.float32) * DIM ** (-0.5)
        w_proj = jax.random.normal(k3, (DIM, DIM), dtype=jnp.float32) * DIM ** (-0.5)
        b_proj = jax.random.normal(k4, (DIM,), dtype=jnp.float32) * 0.02
        bias_table = jax.random.normal(k5, ((2 * WS - 1) ** 2, NH), dtype=jnp.float32) * 0.02
        rel_index = _rel_index(WS)
        return {'x': x, 'w_qkv': w_qkv, 'w_proj': w_proj, 'b_proj': b_proj, 'bias_table': bias_table, 'rel_index': rel_index}
    _L0_conv_all = _L0_conv_setup()
    _L0_conv_in = {k: v for k, v in _L0_conv_all.items() if k in ('w_qkv', 'w_proj', 'b_proj', 'bias_table', 'rel_index')}
    del _L0_conv_all

    def _L1_conv_setup():
        import jax, jax.numpy as jnp
        from jax import lax
        import numpy as np
        H, W = (32, 32)
        K = 5
        SIGMA = 0.5
        CHAN_PER_POS = 8
        INIT_STRIDE = 16
        BATCH = 32

        def _num_offsets(h, w, s):
            ny = (h - s) // s * 2 + 1
            nx = (w - s) // s * 2 + 1
            return (ny, nx, ny * nx - 1)

        def _displace(x, off_int):
            _, _, _, h, w = x.shape

            def shift_one(xp, dxy):
                dx, dy = (dxy[0], dxy[1])
                ys = jnp.arange(h) - dy
                xs = jnp.arange(w) - dx
                ym = (ys >= 0) & (ys < h)
                xm = (xs >= 0) & (xs < w)
                ysc = jnp.clip(ys, 0, h - 1)
                xsc = jnp.clip(xs, 0, w - 1)
                out = xp[:, :, ysc][:, :, :, xsc]
                return out * (ym[:, None] & xm[None, :]).astype(xp.dtype)
            return jax.vmap(shift_one, in_axes=(1, 0), out_axes=1)(x, off_int)
        key = jax.random.key(seed)
        k1, k2 = jax.random.split(key)
        ny, nx, npos = _num_offsets(H, W, INIT_STRIDE)
        C = npos * CHAN_PER_POS
        x = jax.random.normal(k1, (BATCH, C, H, W), dtype=jnp.float32)
        offs = []
        for ih in range(-(ny // 2), ny // 2 + 1):
            for iw in range(-(nx // 2), nx // 2 + 1):
                if ih == 0 and iw == 0:
                    continue
                offs.append([iw * INIT_STRIDE, ih * INIT_STRIDE])
        offset = jnp.asarray(np.array(offs, dtype=np.float32))
        offset = offset + jax.random.uniform(k2, offset.shape, dtype=jnp.float32, minval=-0.4, maxval=0.4)
        return {'x': x, 'offset': offset}
    _L1_conv_all = _L1_conv_setup()
    _L1_conv_in = {k: v for k, v in _L1_conv_all.items() if k in ('offset',)}
    del _L1_conv_all
    return {'x': x, 'L0_conv_w_qkv': _L0_conv_in['w_qkv'], 'L0_conv_w_proj': _L0_conv_in['w_proj'], 'L0_conv_b_proj': _L0_conv_in['b_proj'], 'L0_conv_bias_table': _L0_conv_in['bias_table'], 'L0_conv_rel_index': _L0_conv_in['rel_index'], 'L1_conv_offset': _L1_conv_in['offset']}

def reference(x, L0_conv_w_qkv, L0_conv_w_proj, L0_conv_b_proj, L0_conv_bias_table, L0_conv_rel_index, L1_conv_offset):
    import jax
    import jax.numpy as jnp

    def _L0_conv_ref(x, w_qkv, w_proj, b_proj, bias_table, rel_index):
        import jax, jax.numpy as jnp
        import numpy as np
        WS, NH = (7, 12)
        DIM, B, H, W = (192, 32, 56, 56)

        def _rel_index(ws):
            coords = np.stack(np.meshgrid(np.arange(ws), np.arange(ws), indexing='ij')).reshape(2, -1)
            rel = (coords[:, :, None] - coords[:, None, :]).transpose(1, 2, 0)
            rel[..., 0] += ws - 1
            rel[..., 1] += ws - 1
            rel[..., 0] *= 2 * ws - 1
            return jnp.asarray(rel.sum(-1), dtype=jnp.int32)
        b, c, h, w = x.shape
        hd = c // NH
        scale = hd ** (-0.5)
        hh, ww = (h // WS, w // WS)
        qkv = jnp.einsum('bchw,oc->bohw', x, w_qkv)
        qkv = qkv.reshape(b, 3, NH, hd, hh, WS, ww, WS)
        qkv = qkv.transpose(1, 0, 4, 6, 2, 5, 7, 3).reshape(3, b * hh * ww, NH, WS * WS, hd)
        q, k, v = (qkv[0], qkv[1], qkv[2])
        bias = bias_table[rel_index].transpose(2, 0, 1)
        dots = jnp.einsum('wnid,wnjd->wnij', q, k) * scale + bias[None]
        attn = jax.nn.softmax(dots, axis=-1)
        out = jnp.einsum('wnij,wnjd->wnid', attn, v)
        out = out.reshape(b, hh, ww, NH, WS, WS, hd).transpose(0, 3, 6, 1, 4, 2, 5).reshape(b, c, h, w)
        out = jnp.einsum('bchw,oc->bohw', out, w_proj) + b_proj[None, :, None, None]
        return out

    def _L1_conv_ref(x, offset):
        import jax, jax.numpy as jnp
        from jax import lax
        import numpy as np
        H, W = (32, 32)
        K = 5
        SIGMA = 0.5
        CHAN_PER_POS = 8
        INIT_STRIDE = 16
        BATCH = 32

        def _num_offsets(h, w, s):
            ny = (h - s) // s * 2 + 1
            nx = (w - s) // s * 2 + 1
            return (ny, nx, ny * nx - 1)

        def _displace(x, off_int):
            _, _, _, h, w = x.shape

            def shift_one(xp, dxy):
                dx, dy = (dxy[0], dxy[1])
                ys = jnp.arange(h) - dy
                xs = jnp.arange(w) - dx
                ym = (ys >= 0) & (ys < h)
                xm = (xs >= 0) & (xs < w)
                ysc = jnp.clip(ys, 0, h - 1)
                xsc = jnp.clip(xs, 0, w - 1)
                out = xp[:, :, ysc][:, :, :, xsc]
                return out * (ym[:, None] & xm[None, :]).astype(xp.dtype)
            return jax.vmap(shift_one, in_axes=(1, 0), out_axes=1)(x, off_int)
        B, C, h, w = x.shape
        P = offset.shape[0]
        cpp = C // P
        off_round = jnp.round(offset)
        off_int = off_round.astype(jnp.int32)
        disp = _displace(x.reshape(B, P, cpp, h, w), off_int).reshape(B, C, h, w)
        sub = offset - lax.stop_gradient(off_round)
        c = K // 2
        jj, ii = jnp.meshgrid(jnp.arange(K, dtype=jnp.float32) - c, jnp.arange(K, dtype=jnp.float32) - c, indexing='xy')
        field = jnp.stack([jj, ii], axis=-1)
        d = field[None] + sub[:, None, None, :]
        kernel = jnp.exp(-jnp.sum(d * d, axis=-1) / (2.0 * SIGMA ** 2))
        kernel = kernel / jnp.sum(kernel, axis=(1, 2), keepdims=True)
        kw = jnp.repeat(kernel, cpp, axis=0)[:, None]
        out = lax.conv_general_dilated(disp, kw, window_strides=(1, 1), padding=[(c, c), (c, c)], feature_group_count=C, dimension_numbers=('NCHW', 'OIHW', 'NCHW'))
        return out

    def _gn(v, G=32, eps=1e-05):
        B_, C_, H_, W_ = v.shape
        g = v.reshape(B_, G, C_ // G, H_, W_)
        m = jnp.mean(g, axis=(2, 3, 4), keepdims=True)
        s = jnp.var(g, axis=(2, 3, 4), keepdims=True)
        return ((g - m) / jnp.sqrt(s + eps)).reshape(v.shape)

    def _ln_c(v, eps=1e-06):
        m = jnp.mean(v, axis=1, keepdims=True)
        s = jnp.var(v, axis=1, keepdims=True)
        return (v - m) / jnp.sqrt(s + eps)

    def _ln_t(v, eps=1e-05):
        m = jnp.mean(v, axis=-1, keepdims=True)
        s = jnp.var(v, axis=-1, keepdims=True)
        return (v - m) / jnp.sqrt(s + eps)

    def _to_tokens(v):
        B_, C_, H_, W_ = v.shape
        return v.reshape(B_, C_, H_ * W_).transpose(0, 2, 1)

    def _from_tokens(t, like):
        B_, C_, H_, W_ = like.shape
        return t.transpose(0, 2, 1).reshape(B_, C_, H_, W_)
    x = x + _L0_conv_ref(_gn(x), L0_conv_w_qkv, L0_conv_w_proj, L0_conv_b_proj, L0_conv_bias_table, L0_conv_rel_index)
    x = x + _L1_conv_ref(_gn(x), L1_conv_offset)
    return x

_drawn_inputs = setup_inputs


def setup_inputs(seed=0):
    import zlib

    import numpy as np

    out = dict(_drawn_inputs(seed))
    spreads = {}
    factors = {'L0_conv_bias_table': 8.0}
    for name, (base, spread) in spreads.items():
        noise = np.random.default_rng([zlib.crc32(name.encode()), seed]).standard_normal(out[name].shape)
        drawn = base * np.exp(spread * noise) if base else spread * noise
        out[name] = jnp.asarray(drawn.astype(out[name].dtype))
    for name, factor in factors.items():
        out[name] = (out[name] * factor).astype(out[name].dtype)
    return out
```

```python
from contextlib import ExitStack

import numpy as np
import concourse.bass as bass
from concourse import mybir

F32 = mybir.dt.float32
F16 = mybir.dt.float16
I32 = mybir.dt.int32
ALU = mybir.AluOpType
ACT = mybir.ActivationFunctionType
AX = mybir.AxisListType

C, HW = 192, 56
CM, CT = 128, 64
WS, NH, HD = 7, 12, 16
NT = WS * WS
NWX = HW // WS
ROW = NWX * NT
TOK = HW * HW
CHUNK = 2 * ROW
NCH = TOK // CHUNK
PAIRS = NWX * NWX // 2
PPC = PAIRS // NCH
PPR = NWX // 2
NHP = NH // 2
QPAD = 16
POS, CPP = 8, C // 8
CC = C // 2
BC = 6
NB = CC // BC
SY = 2 * HW
WSC = 256.0
PSC = 1024.0
ASC = 64.0
GROUPS = 32
CPG = C // GROUPS
EPS = 1e-5
TAPS, SIGMA = 5, 0.5
ROUND = 1.5 * 2.0 ** 23
FAR = 2.0 ** 20
NREL = (2 * WS - 1) ** 2

CF = {}
_at = 0
for _n, _w in (("ident", 128), ("gmm", 128), ("gtm", 128), ("gmt", 128), ("gtt", 128), ("lm", SY),
               ("sm", CM // 2), ("kmask", 2), ("u0", HW), ("ys", 1), ("smask", 2),
               ("taps", TAPS), ("iota", 2)):
    CF[_n] = (_at, _at + _w)
    _at += _w
NCF = _at
KEEP = CF["u0"][0]


def constants():
    f = np.zeros((128, NCF), np.float32)
    p = np.arange(128)

    def put(name, a):
        f[:a.shape[0], CF[name][0]:CF[name][1]] = a

    put("ident", np.eye(128))
    gm, gt = p // CPG, (CM + p % CT) // CPG
    put("gmm", (gm[:, None] == gm[None]) / CPG)
    put("gtm", (gt[:, None] == gm[None]) / (2 * CPG))
    put("gmt", (gm[:, None] == gt[None]) / CPG)
    put("gtt", (gt[:, None] == gt[None]) / (2 * CPG))
    put("lm", p[:, None] % 2 == np.arange(SY)[None] // HW)
    put("sm", p[:, None] // 2 == np.arange(CM // 2)[None])
    put("kmask", np.stack([p // HD % 2 == 0, p // HD % 2 == 1], 1) / WSC)
    put("u0", (p[:SY, None] % HW) - np.arange(HW)[None])
    put("ys", p[:SY, None] % HW)
    put("smask", np.stack([p < HW, (p >= HW) & (p < SY)], 1)[:SY])
    put("taps", np.tile(np.arange(TAPS) - TAPS // 2, (128, 1)))
    put("iota", np.stack([p, p + 128], 1))
    h = np.zeros((128, 128), np.float16)
    h[(p[:, None] % 64 == p[None] % 64) & (p[:, None] % 64 < NT)] = 1
    return f, h


class Image:

    def __init__(self, base, shift=0):
        self.base, self.shift = base, shift

    def __add__(self, n):
        return Image(self.base, self.shift + n)

    def __sub__(self, n):
        return self + -n

    def row(self):
        return self.base + self.shift


SET_HOT, SET_GAUSS, SET_ALL = 5, 23, 42


def build(nc, x, w_in, b_out, table, rel, offset, cf, ch, scratch, out):
    images = x.shape[0]
    ctx = ExitStack()
    with ctx:
        def sb(name, shape, dt):
            return ctx.enter_context(nc.sbuf_tensor(name, shape, dt))

        def pb(name, shape):
            return ctx.enter_context(nc.psum_tensor(name, shape, F32))

        def sem(name):
            return ctx.enter_context(nc.semaphore(name))

        xm = sb("xm", [128, 2, TOK], F32)
        xt = sb("xt", [128, 2, TOK // 2], F32)
        xnh = sb("xnh", [128, 2 * CHUNK], F16)
        xnl = sb("xnl", [128, 2 * CHUNK], F16)
        xnt = sb("xnt", [128, 2 * CHUNK], F16)
        xnf = sb("xnf", [128, 2, ROW], F32)
        qks = sb("qks", [128, 6, CHUNK], F16)
        mix = sb("mix", [128, 4, CHUNK], F16)
        kst = sb("kst", [96, 2, NHP, 2, CHUNK], F16)
        qst = sb("qst", [96, 2, NHP * CHUNK + QPAD], F16)
        prob = sb("prob", [128, 2, NH * NT], F32)
        probn = sb("probn", [128, 2, NH * NT], F32)
        pT = sb("pT", [128, 2, 2, NH, NT], F16)
        cv = sb("cv", [98, 2, PPR, 2, C], F16)
        vv = sb("vv", [98, 2, 2, PPR, 2, C], F16)
        om = sb("om", [128, 2, 2, ROW], F16)
        ot = sb("ot", [128, 2, ROW], F16)
        pjt = sb("pjt", [128, 2, ROW], F32)
        wmh = sb("wmh", [128, 4 * C], F16)
        wml = sb("wml", [128, 4 * C], F16)
        wth = sb("wth", [128, 4 * C], F16)
        wtl = sb("wtl", [128, 4 * C], F16)
        bp = sb("bp", [128, 2], F32)
        biasT = sb("biasT", [128, NH * NT], F16)
        xr = sb("xr", [SY, CC * HW], F32)
        xcf = sb("xcf", [128, 2, BC * HW], F32)
        xc = sb("xc", [SY, 2, 2, BC * HW], F16)
        z = sb("z", [SY, 2, 2, 3 * SY], F16)
        amat = sb("amat", [SY, 2, 2 * POS, SY], F16)
        cst = sb("cst", [128, KEEP], F32)
        addb = sb("addb", [128, 128], F16)
        mx = sb("mx", [128, 2, NH], F32)
        den = sb("den", [128, 2, NH], F32)
        gst = [sb(f"gst{n}", [128, 12, 6], F32) for n in (1, 2)]
        gmv = [sb(f"gmv{n}", [128, 2, 2], F32) for n in (1, 2)]
        gmean = [sb(f"gmean{n}", [128, 2], F32) for n in (1, 2)]
        gd = [sb(f"gd{n}", [128, 2], F32) for n in (1, 2)]
        gv = [sb(f"gv{n}", [128, 2], F32) for n in (1, 2)]
        gve = [sb(f"gve{n}", [128, 2], F32) for n in (1, 2)]
        grs = [sb(f"grs{n}", [128, 2], F32) for n in (1, 2)]
        mhalf = sb("mhalf", [128, 2], F32)
        gnb = sb("gnb", [128, 2], F32)
        coef = sb("coef", [SY, 2, CC], F32)

        cmain, ctail = (xcf[0:n, b, 0:n].rearrange("p (a c) -> p a c", a=2)
                        for b, n in ((0, CM), (1, CT)))

        def const(name, rows=128):
            a, b = CF[name]
            return cst[0:rows, a:b] if b <= KEEP else cset[0:rows, a - KEEP:b - KEEP]

        pS = pb("pS", [128, 2, 512])
        pT_ = pb("pTr", [128, 1024])
        pO = pb("pO", [128, 2, 2, 128])
        pV = pb("pV", [128, 512])
        pQ = pb("pQ", [128, 512])
        pM = pb("pM", [128, 512])

        S = {n: sem(n) for n in (
            "const_in", "setup", "setup_act", "setup_pe",
            "x_in", "x1_out", "xr_in", "y_out", "stack0", "stack1", "vst0", "vst1",
            "gn1_bn", "gn2_bn", "gn1_dve", "gn1_pe", "gn1_pool", "gn2_dve", "gn2_pe", "gn2_pool",
            "xnf_d", "xnh_a", "xnl_p", "xtl_d",
            "qk_pe", "qk_act", "qk_dve", "v_pe", "v_act", "v_dve",
            "s_pe", "max_d", "sub_d", "exp_a", "sum_d", "rden_d", "norm_p",
            "t_pe", "t_act", "t_dve", "o_pe", "o_act", "o_dve",
            "pj_pe", "pj_act", "x1_p", "xcm_p", "xcf_p", "xch_a", "xcl_p",
            "c1_pe", "z_act", "z_dve", "c2_pe", "y_dve")}
        PER = {"x_in": 48, "x1_out": 48, "xr_in": 32, "y_out": 8 * 16, "stack0": 36 * 16 * 2,
               "stack1": 36 * 16 * 2, "gn1_bn": 12, "gn2_bn": 12, "gn1_dve": 7, "gn1_pe": 2, "gn1_pool": 1,
               "gn2_dve": 13, "gn2_pe": 3, "gn2_pool": 1, "xnf_d": 16, "xnh_a": 16, "xnl_p": 8,
               "xtl_d": 8, "qk_pe": 24, "qk_act": 24, "qk_dve": 24, "pj_pe": 16, "pj_act": 16,
               "x1_p": 16, "o_act": 16, "o_dve": 16}
        PER.update(v_pe=16, v_act=16, v_dve=16, vst0=256, vst1=256)
        for n in ("s_pe", "max_d", "sub_d", "exp_a", "sum_d", "rden_d",
                  "norm_p", "t_pe", "t_act", "t_dve", "o_pe"):
            PER[n] = PAIRS
        for n in ("xcm_p", "xcf_p", "xch_a", "xcl_p", "c1_pe", "z_act", "z_dve", "c2_pe", "y_dve"):
            PER[n] = NB

        def nth(name, i, k):
            return i.base * PER[name] + (i.shift * PER[name] + k)

        def due(name, i, k):
            first = i.base if isinstance(i.base, int) else 1
            return (first + i.shift) * PER[name] + k > 0

        def par(i):
            return (i.base + (i.shift + 2)) % 2

        def windows(ap):
            return ap.rearrange("p (yi wx xi) -> p wx yi xi", yi=WS, wx=NWX)

        def wmajor(ap):
            return ap.rearrange("p (wx yi xi) -> p wx yi xi", yi=WS, wx=NWX)

        def heads(ap):
            return ap.rearrange("p (h j) -> p h j", j=NT)

        def spread(ap, n):
            return ap.rearrange("p (a o) -> p a o", o=1).to_broadcast([ap.shape[0], ap.shape[1], n])

        def norm_step(p, att, nxt):
            for lo, shift, c, on in ((4, 0, 2, att), (12, 0, 3, att), (20, 1, 0, nxt), (28, 1, 1, nxt)):
                if on and lo <= p < lo + 4:
                    return shift, c, p - lo
            return None

        def qk_steps(p, att, nxt):
            c, q = divmod(p, PPC)
            shift, cn = (0, c + 1) if c + 1 < NCH else (1, 0)
            if q < 3 and (nxt if shift else att):
                return shift, cn, (2 * q, 2 * q + 1)
            return None

        def v_step(p, att, nxt):
            if p % 2 == 0 and (att if p + PPR < PAIRS else nxt):
                return (p + PPR) // PAIRS, (p + PPR) % PAIRS // 2
            return None

        def v_out(step, part):
            k = 2 * (step % 2)
            return cv[:, step // 2 % 2, k:k + 2, part, :]

        def proj_step(p, prev, att):
            for r in range(NWX):
                for tail in (0, 1):
                    s = PPR * r + 7 + tail
                    if s == p and att:
                        return 0, r, tail
                    if s - PAIRS == p and prev:
                        return -1, r, tail
            return None

        def blur_step(p, first, prev):
            return p - first if prev and 0 <= p - first < NB else None

        cset = probn[:, 1, 0:NCF - KEEP]
        tabs = probn[:, 0, 0:2 * NH].rearrange("p (a h) -> p a h", a=2)
        tabh = probn[:, 0, 2 * NH:4 * NH].bitcast(F16).rearrange("p (b a h) -> p b a h", a=2, b=2)
        hot = [b[:, :, :].rearrange("p a t -> p (a t)") for b in (qks, mix)]
        dist = xr[:, 0:2 * POS * HW].rearrange("p (a y) -> p a y", y=HW)
        gauss = xr[:, 2 * POS * HW:4 * POS * HW].rearrange("p (a y) -> p a y", y=HW)
        tapv = xr[:, 4 * POS * HW:4 * POS * HW + 2 * POS * TAPS].rearrange("p (a t) -> p a t", t=TAPS)

        def hot_out(bank):
            return bank[:, :, :] if bank is pS else bank[:, :].rearrange("p (b c) -> p b c", b=2)

        def turned():
            return pT_[0:2 * NT, 0:128 * NHP].rearrange("p (q s) -> p q s", s=64)[:, :, 0:NT]

        def pairs2(ap):
            return ap.rearrange("p (a t) -> p a t", a=2)

        block = ctx.enter_context(nc.Block())

        def bodies(eng, body):
            body(Image(-1), False, False, True)
            body(Image(0), False, True, True)
            if images > 2:
                with eng.Fori(1, images - 1) as i:
                    body(Image(i), True, True, True)
            body(Image(images - 1), True, True, False)
            body(Image(images), True, False, False)

        @block.sync
        def _(sp):
            sp.dma_start(cst[:, :], cf[:, 0:KEEP]).then_inc(S["const_in"], 16)
            sp.dma_start(cset, cf[:, KEEP:NCF]).then_inc(S["const_in"], 16)
            sp.dma_start(addb[:, :], ch).then_inc(S["const_in"], 16)
            sp.dma_start(xm[:, 0, 0:4 * C], w_in[0:CM, :]).then_inc(S["const_in"], 16)
            sp.dma_start(xm[0:64, 0, 4 * C:8 * C], w_in[CM:C, :]).then_inc(S["const_in"], 16)
            sp.dma_start(xm[64:128, 0, 4 * C:8 * C], w_in[CM:C, :]).then_inc(S["const_in"], 16)
            sp.dma_start(bp[:, 0:1], b_out[0:CM, :]).then_inc(S["const_in"], 16)
            sp.dma_start(bp[0:64, 1:2], b_out[CM:C, :]).then_inc(S["const_in"], 16)
            sp.dma_start(bp[64:128, 1:2], b_out[CM:C, :]).then_inc(S["const_in"], 16)
            sp.dma_start(tabs[:, 0, :], table[0:128, :]).then_inc(S["const_in"], 16)
            sp.wait_ge(S["setup"], 1)
            sp.dma_start(tabs[0:NREL - 128, 1, :], table[128:NREL, :]).then_inc(S["const_in"], 16)
            sp.dma_start(xm[:, 1, 0:NT * NT].bitcast(I32),
                         rel.rearrange("(o i) j -> o (i j)", o=1).to_broadcast([128, NT * NT])).then_inc(S["const_in"], 16)
            sp.dma_start(xt[0:SY, 0, 0:2 * POS], offset.rearrange("(o q) a -> o (q a)", o=1)
                         .to_broadcast([SY, 2 * POS])).then_inc(S["const_in"], 16)

            def stack(i, c, blk):
                buf, done = c % 2, S[f"stack{c % 2}"]
                sp.wait_ge(S["qk_dve"], nth("qk_dve", i, 6 * c + 2 * blk + 2))
                if blk != 1:
                    src = qks if blk == 0 else mix
                    for n, hp in enumerate(range(4) if blk == 0 else range(4, NHP)):
                        for r, part in enumerate((0, 1, 0)):
                            sp.dma_start(qst[32 * r:32 * r + 32, buf, CHUNK * hp:CHUNK * hp + CHUNK],
                                         src[32 * n:32 * n + 32, part, :]).then_inc(done, 16)
                if blk != 0:
                    src, row, at = (qks, 0, 2) if blk == 1 else (mix, 64, 0)
                    for n, hp in enumerate(range(4) if blk == 1 else range(4, NHP)):
                        for r, part in enumerate((0, 0, 1)):
                            sp.dma_start(kst[32 * r:32 * r + 32, buf, hp, :, :],
                                         src[row + 32 * n:row + 32 * n + 32,
                                             at + 2 * part:at + 2 * part + 2, :]).then_inc(done, 16)

            def spread_v(i, g):
                sp.wait_ge(S["v_dve"], nth("v_dve", i, 2 * g + 2))
                for w in (0, 1):
                    for a in (0, 1):
                        h = slice(C // 2 * a, C // 2 * a + C // 2)
                        src = cv[NT * w:NT * w + NT, g % 2, :, :, h].rearrange("j p b c -> j (p b) c")
                        dst = vv[NT * a:NT * a + NT, g % 2, w, :, :, h].rearrange("j p b c -> j (p b) c")
                        sp.dma_start(dst, src).then_inc(S[f"vst{g % 2}"], 16)

            def body(i, prev, att, nxt):
                for p in range(PAIRS):
                    qk = qk_steps(p - 1, att, nxt) if p % PPC else None
                    if qk:
                        shift, c, groups = qk
                        stack(i + shift, c, groups[0] // 2)
                    v = v_step(p - 1, att, nxt) if p % PPR == PPR - 1 else None
                    if v:
                        spread_v(i + v[0], v[1] // 2)
                    if p == 6 and prev:
                        sp.wait_ge(S["x1_p"], nth("x1_p", i, 0))
                        sp.dma_start(scratch[0:CM, :], xm[:, par(i - 1), :]).then_inc(S["x1_out"], 16)
                        if due("y_out", i - 1, 0):
                            sp.wait_ge(S["y_out"], nth("y_out", i - 1, 0))
                        for h in (0, 1):
                            sp.dma_start(scratch[CM:C, h * (TOK // 2):(h + 1) * (TOK // 2)],
                                         xt[64 * h:64 * h + 64, par(i - 1), :]).then_inc(S["x1_out"], 16)
                        sp.wait_ge(S["x1_out"], nth("x1_out", i, 0))
                        v = scratch.rearrange("(c s) (y x) -> s y c x", s=2, x=HW)
                        for s in (0, 1):
                            sp.dma_start(xr[HW * s:HW * s + HW, :].rearrange(
                                "y (c x) -> y c x", x=HW), v[s]).then_inc(S["xr_in"], 16)
                    if p == 7 and nxt:
                        if due("gn2_bn", i - 1, 12):
                            sp.wait_ge(S["gn2_bn"], nth("gn2_bn", i - 1, 12))
                        if not att:
                            sp.wait_ge(S["setup"], SET_ALL)
                        xi = x[(i + 1).row()].rearrange("c y x -> c (y x)")
                        sp.dma_start(xm[:, par(i + 1), :], xi[0:CM, :]).then_inc(S["x_in"], 16)
                        for h in (0, 1):
                            sp.dma_start(xt[64 * h:64 * h + 64, par(i + 1), :],
                                         xi[CM:C, h * (TOK // 2):(h + 1) * (TOK // 2)]).then_inc(S["x_in"], 16)
                    b = blur_step(p, 15, prev)
                    if b is not None and b % 4 == 3:
                        sp.wait_ge(S["y_dve"], nth("y_dve", i - 1, b + 1))
                        c = slice(b // 4 * CPP, b // 4 * CPP + CPP)
                        v = out[(i - 1).row()].rearrange("(c s) y x -> s y c x", s=2)
                        for s in (0, 1):
                            src = xr[HW * s:HW * s + HW, :].rearrange("y (c x) -> y c x", x=HW)
                            sp.dma_start(v[s][:, c], src[:, c]).then_inc(S["y_out"], 16)

            bodies(sp, body)
            sp.wait_ge(S["y_out"], images * PER["y_out"])

        @block.tensor
        def _(pe):
            def three(out_ap, lh, ll, rh, rl, start=True, stop=True):
                pe.matmul(out_ap, lh, rh, start=start, stop=False, skip_group_check=True)
                pe.matmul(out_ap, ll, rh, start=False, stop=False, skip_group_check=True)
                return pe.matmul(out_ap, lh, rl, start=False, stop=stop, skip_group_check=True)

            pe.wait_ge(S["setup"], SET_HOT)
            for part, bank in ((0, pT_), (1, pS)):
                for j in range(NT):
                    o = hot_out(bank)[0:NT, (j // 42), NH * (j % 42):NH * (j % 42) + NH]
                    for half, rows in ((0, 128), (1, NREL - 128)):
                        lhs = hot[half][0:rows, 0:NT * NT].rearrange("p (i j) -> p j i", j=NT)[:, j, :]
                        mm = pe.matmul(o, lhs, tabh[0:rows, part, half, :], start=(half == 0),
                                       stop=(half == 1), skip_group_check=True)
            mm.then_inc(S["setup_pe"], 1)
            pe.wait_ge(S["setup"], SET_ALL)

            def group_sum(n, o, src):
                for col, (a, b) in enumerate((("gmm", "gtm"), ("gmt", "gtt"))):
                    pe.matmul(o[:, col:col + 1], const(a), src[:, 0:1], start=True, stop=False,
                              skip_group_check=True)
                    mm = pe.matmul(o[:, col:col + 1], const(b), src[:, 1:2], start=False, stop=True,
                                   skip_group_check=True)
                return mm

            def qk(i, c, g):
                if due("qk_dve", i, 6 * c + g):
                    pe.wait_ge(S["qk_dve"], nth("qk_dve", i, 6 * c + g))
                row = 2 * c + g % 2
                pe.wait_ge(S["xnh_a"], nth("xnh_a", i, 4 * c + 4))
                pe.wait_ge(S["xnl_p"], nth("xnl_p", i, 2 * c + 2))
                pe.wait_ge(S["xtl_d"], nth("xtl_d", i, 2 * c + 2))
                w, t, o = slice(128 * (g // 2), 128 * (g // 2) + 128), slice(ROW * (row % 4), ROW * (row % 4) + ROW), pQ[:, 0:ROW]
                three(o, wmh[:, w], wml[:, w], xnh[:, t], xnl[:, t], stop=False)
                pe.matmul(o, wth[:, w], xnt[:, t], start=False, stop=False, skip_group_check=True)
                pe.matmul(o, wtl[0:64, w], xnt[0:64, t], start=False, stop=True,
                          skip_group_check=True).then_inc(S["qk_pe"], 1)

            def values(i, step):
                if due("v_dve", i, step):
                    pe.wait_ge(S["v_dve"], nth("v_dve", i, step))
                c = 2 * step // PPC
                pe.wait_ge(S["xnh_a"], nth("xnh_a", i, 4 * c + 4))
                pe.wait_ge(S["xnl_p"], nth("xnl_p", i, 2 * c + 2))
                pe.wait_ge(S["xtl_d"], nth("xtl_d", i, 2 * c + 2))
                w = slice(3 * 128, 3 * 128 + C)
                for k in (0, 1):
                    at = 2 * NT * ((2 * step + k) % (2 * PPC))
                    t, o = slice(at, at + 2 * NT), pV[0:2 * NT, C * k:C * k + C]
                    three(o, xnh[:, t], xnl[:, t], wmh[:, w], wml[:, w], stop=False)
                    pe.matmul(o, xnt[:, t], wth[:, w], start=False, stop=False, skip_group_check=True)
                    mm = pe.matmul(o, xnt[0:64, t], wtl[0:64, w], start=False, stop=True,
                                   skip_group_check=True)
                mm.then_inc(S["v_pe"], 1)

            def scores(i, p):
                c, q = divmod(p, PPC)
                if q == 0:
                    pe.wait_ge(S[f"stack{c % 2}"], nth(f"stack{c % 2}", i, 576 * (c // 2 + 1)))
                if due("sub_d", i, p):
                    pe.wait_ge(S["sub_d"], nth("sub_d", i, p))
                for half in (0, 1):
                    pe.matmul(pS[:, half, 0:294], addb[:, :], biasT[:, 294 * half:294 * half + 294],
                              start=True, stop=False, skip_group_check=True)
                for win in (0, 1):
                    t = NT * (2 * q + win)
                    for hp in range(NHP):
                        o = pS[64 * win:64 * win + 64, hp // 3, 98 * (hp % 3):98 * (hp % 3) + 98]
                        mm = pe.matmul(o.rearrange("p (a j) -> p a j", a=2), qst[:, c % 2, CHUNK * hp + t:CHUNK * hp + t + 64],
                                       kst[:, c % 2, hp, :, t:t + NT], start=False, stop=True,
                                       skip_group_check=True)
                mm.then_inc(S["s_pe"], 1)

            def turn(i, p):
                pe.wait_ge(S["norm_p"], nth("norm_p", i, p + 1))
                if due("t_dve", i, p):
                    pe.wait_ge(S["t_dve"], nth("t_dve", i, p))
                for hp in range(NHP):
                    mm = pe.transpose(pT_[0:98, 128 * hp:128 * hp + 128],
                                      probn[:, p % 2, 98 * hp:98 * hp + 98], const("ident"))
                mm.then_inc(S["t_pe"], 1)

            def attend(i, p):
                pe.wait_ge(S["t_dve"], nth("t_dve", i, p + 1))
                g = p // PPR
                pe.wait_ge(S[f"vst{g % 2}"], nth(f"vst{g % 2}", i, 64 * (g // 2 + 1)))
                if p % 2 == 0:
                    if due("o_dve", i, p // 2):
                        pe.wait_ge(S["o_dve"], nth("o_dve", i, p // 2))
                for win in (0, 1):
                    for hps in (range(4), range(4, NHP)):
                        for k, (a, b) in enumerate(((0, 0), (1, 0), (0, 1))):
                            for hp in hps:
                                r = 32 * (hp % 4)
                                mm = pe.matmul(pO[r:r + 32, p % 2, hp // 4, NT * win:NT * win + NT],
                                               vv[:, g % 2, win, p % PPR, a, hp::NHP],
                                               pT[0:98, p % 2, b, 2 * hp + win, :],
                                               start=(k == 0), stop=(k == 2), skip_group_check=True)
                mm.then_inc(S["o_pe"], 1)

            def project(i, r, tail):
                if due("pj_act", i, 2 * r + tail):
                    pe.wait_ge(S["pj_act"], nth("pj_act", i, 2 * r + tail))
                pe.wait_ge(S["o_dve"], nth("o_dve", i, 2 * r + 2))
                n = CT if tail else CM
                w, o = slice(3 * C + CM * tail, 3 * C + CM * tail + n), pM[0:n, 0:ROW]
                w = slice(w.start, w.start + n)
                three(o, wmh[:, w], wml[:, w], om[:, r % 2, 0, :], om[:, r % 2, 1, :], stop=False)
                pe.matmul(o, wth[:, w], ot[:, r % 2, :], start=False, stop=False, skip_group_check=True)
                pe.matmul(o, wtl[0:64, w], ot[0:64, r % 2, :], start=False, stop=True,
                          skip_group_check=True).then_inc(S["pj_pe"], 1)

            def blur(i, b, stage):
                if stage == 0:
                    if b == 1:
                        pe.wait_ge(S["z_dve"], nth("z_dve", i, b))
                    if b > 1:
                        pe.wait_ge(S["y_dve"], nth("y_dve", i, b - 1))
                    pe.wait_ge(S["xcl_p"], nth("xcl_p", i, b + 1))
                    src = xc
                else:
                    if b < NB - 1:
                        pe.wait_ge(S["z_dve"], nth("z_dve", i, b + 2))
                    else:
                        pe.wait_ge(S["y_dve"], nth("y_dve", i, b))
                    pe.wait_ge(S["z_dve"], nth("z_dve", i, b + 1))
                    src = z
                m = 2 * (b // (CPP // 2 // BC)) + (1 if stage == 0 else 0)
                for j in range(BC // 2):
                    k = slice(SY * j, SY * j + SY)
                    mm = three(pM[0:SY, k], src[:, b % 2, 0, k], src[:, b % 2, 1, k],
                               amat[:, 0, m, :], amat[:, 1, m, :])
                mm.then_inc(S["c1_pe" if stage == 0 else "c2_pe"], 1)

            def body(i, prev, att, nxt):
                for p in range(PAIRS):
                    if att:
                        scores(i, p)
                    if p >= 2 and att or p < 2 and prev:
                        attend(i if p >= 2 else i - 1, (p - 2) % PAIRS)
                    q = qk_steps(p, att, nxt)
                    if nxt and p in (18, 24):
                        pe.wait_ge(S["gn1_dve"], nth("gn1_dve", i + 1, 3 if p == 18 else 7))
                    if q:
                        qk(i + q[0], q[1], q[2][0])
                    if p >= 1 and att or p < 1 and prev:
                        turn(i if p >= 1 else i - 1, (p - 1) % PAIRS)
                    v = v_step(p, att, nxt)
                    if v:
                        values(i + v[0], v[1])
                    if q:
                        qk(i + q[0], q[1], q[2][1])
                    pj = proj_step(p, prev, att)
                    if pj and prev and p == 8:
                        pe.wait_ge(S["gn2_dve"], nth("gn2_dve", i - 1, 3))
                    if pj and prev and p == 11:
                        pe.wait_ge(S["gn2_dve"], nth("gn2_dve", i - 1, 13))
                    if pj and prev and p >= 15:
                        pe.wait_ge(S["y_dve"], nth("y_dve", i - 1, min(p - 14, NB)))
                    if pj:
                        project(i + pj[0], pj[1], pj[2])
                    b = blur_step(p, 13, prev)
                    if b == 0:
                        pe.wait_ge(S["gn2_dve"], nth("gn2_dve", i - 1, 13))
                    if b is not None and (pj or b == 0) and att:
                        n = 2 * pj[1] + pj[2] + 1 if pj else 4
                        pe.wait_ge(S["pj_act"], nth("pj_act", i, n))
                    if b is not None:
                        blur(i - 1, b, 0)
                    b = blur_step(p, 14, prev)
                    if b is not None:
                        blur(i - 1, b, 1)
                    if nxt and p == 17:
                        if att:
                            pe.wait_ge(S["qk_dve"], nth("qk_dve", i, 6 * 3 + 4))
                        pe.wait_ge(S["gn1_dve"], nth("gn1_dve", i + 1, 2))
                        group_sum(1, pQ, gmv[0][:, :, 0]).then_inc(S["gn1_pe"], 1)
                    if nxt and p == 18:
                        if att:
                            pe.wait_ge(S["qk_dve"], nth("qk_dve", i, 6 * 3 + 6))
                        pe.wait_ge(S["gn1_dve"], nth("gn1_dve", i + 1, 6))
                        group_sum(1, pQ, gv[0]).then_inc(S["gn1_pe"], 1)
                    if prev and p == 7:
                        pe.wait_ge(S["pj_act"], nth("pj_act", i - 1, 17 if att else 16))
                        pe.wait_ge(S["gn2_dve"], nth("gn2_dve", i - 1, 2))
                        group_sum(2, pM, gmv[1][:, :, 0]).then_inc(S["gn2_pe"], 1)
                    if prev and p == 8:
                        if att:
                            pe.wait_ge(S["pj_act"], nth("pj_act", i, 2))
                        pe.wait_ge(S["gn2_dve"], nth("gn2_dve", i - 1, 6))
                        group_sum(2, pM, gv[1]).then_inc(S["gn2_pe"], 1)
                    if prev and p == 10:
                        pe.wait_ge(S["gn2_dve"], nth("gn2_dve", i - 1, 12))
                        o = pM[0:SY, 0:2 * CC].rearrange("p (a c) -> p a c", a=2)
                        pe.matmul(o[:, :, 0:CM // 2], const("lm"), cmain, start=True, stop=True,
                                  skip_group_check=True)
                        pe.matmul(o[:, :, CM // 2:CC], const("lm", CT), ctail, start=True, stop=True,
                                  skip_group_check=True).then_inc(S["gn2_pe"], 1)


            bodies(pe, body)

        @block.scalar
        def _(act):
            act.wait_ge(S["setup"], SET_GAUSS)
            act.activation(gauss, gauss, ACT.Exp, scale=-1.0 / (2 * SIGMA ** 2)).then_inc(S["setup_act"], 1)
            act.activation(tapv, tapv, ACT.Exp, scale=-1.0 / (2 * SIGMA ** 2)).then_inc(S["setup_act"], 1)
            act.wait_ge(S["setup"], SET_ALL)

            def norm_hi(i, c, s):
                row, tail = 2 * c + s % 2, s // 2
                act.wait_ge(S["xnf_d"], nth("xnf_d", i, 4 * c + s + 1))
                if due("v_pe", i, PPC // 2 * (c - 1)):
                    act.wait_ge(S["v_pe"], nth("v_pe", i, PPC // 2 * (c - 1)))
                if due("qk_pe", i, 6 * (c - 1)):
                    act.wait_ge(S["qk_pe"], nth("qk_pe", i, 6 * (c - 1)))
                t = slice(ROW * (row % 4), ROW * (row % 4) + ROW)
                if tail:
                    act.copy(xnt[0:64, t], xnf[0:64, s % 2, :]).then_inc(S["xnh_a"], 1)
                else:
                    act.copy(xnh[:, t], xnf[:, s % 2, :]).then_inc(S["xnh_a"], 1)

            def qk_hi(i, c, g):
                act.wait_ge(S["qk_pe"], nth("qk_pe", i, 6 * c + g + 1))
                if g == 0:
                    if due(f"stack{(c + 1) % 2}", *((i, 576 * ((c - 1) // 2 + 1)) if c else (i, 0))):
                        act.wait_ge(S[f"stack{(c + 1) % 2}"], nth(f"stack{(c + 1) % 2}", *((i, 576 * ((c - 1) // 2 + 1)) if c else (i, 0))))
                blk, t = g // 2, slice(ROW * (g % 2), ROW * (g % 2) + ROW)
                qs = HD ** -0.5 / WSC
                if blk == 0:
                    act.activation(qks[:, 0, t], pQ[:, 0:ROW], ACT.Copy, scale=qs).then_inc(S["qk_act"], 1)
                elif blk == 1:
                    act.activation(qks[:, 2, t], pQ[:, 0:ROW], ACT.Copy, scale=const("kmask")[:, 0:1])
                    act.activation(qks[:, 3, t], pQ[:, 0:ROW], ACT.Copy,
                                   scale=const("kmask")[:, 1:2]).then_inc(S["qk_act"], 1)
                else:
                    act.activation(mix[0:64, 0, t], pQ[0:64, 0:ROW], ACT.Copy, scale=qs)
                    act.activation(mix[64:128, 0, t], pQ[64:128, 0:ROW], ACT.Copy,
                                   scale=const("kmask")[64:128, 0:1])
                    act.activation(mix[64:128, 1, t], pQ[64:128, 0:ROW], ACT.Copy,
                                   scale=const("kmask")[64:128, 1:2]).then_inc(S["qk_act"], 1)

            def v_hi(i, step):
                act.wait_ge(S["v_pe"], nth("v_pe", i, step + 1))
                g = step // 2
                if due(f"vst{g % 2}", i, 64 * (g // 2)):
                    act.wait_ge(S[f"vst{g % 2}"], nth(f"vst{g % 2}", i, 64 * (g // 2)))
                act.activation(v_out(step, 0), pairs2(pV[0:98, 0:2 * C]), ACT.Copy,
                               scale=1.0 / WSC).then_inc(S["v_act"], 1)

            def exp(i, p):
                act.wait_ge(S["sub_d"], nth("sub_d", i, p + 1))
                act.activation(prob[:, p % 2, :], prob[:, p % 2, :], ACT.Exp).then_inc(S["exp_a"], 1)

            def turned_hi(i, p):
                act.wait_ge(S["t_pe"], nth("t_pe", i, p + 1))
                if due("o_pe", i, p - 1):
                    act.wait_ge(S["o_pe"], nth("o_pe", i, p - 1))
                act.activation(pT[0:98, p % 2, 0], turned(), ACT.Copy, scale=PSC).then_inc(S["t_act"], 1)

            def out_hi(i, k):
                act.wait_ge(S["o_pe"], nth("o_pe", i, 2 * k + 2))
                r = k // 2
                if k % 2 == 0:
                    if due("pj_pe", i, 2 * (r - 1)):
                        act.wait_ge(S["pj_pe"], nth("pj_pe", i, 2 * (r - 1)))
                t = slice(196 * (k % 2), 196 * (k % 2) + 196)
                act.activation(pairs2(om[:, r % 2, 0, t]), pO[:, :, 0, 0:98], ACT.Copy, scale=1.0 / PSC)
                act.activation(pairs2(ot[0:64, r % 2, t]), pO[0:64, :, 1, 0:98], ACT.Copy,
                               scale=1.0 / PSC).then_inc(S["o_act"], 1)

            def project_out(i, r, tail):
                act.wait_ge(S["pj_pe"], nth("pj_pe", i, 2 * r + tail + 1))
                if due("x1_p", i, 2 * r + tail - 1):
                    act.wait_ge(S["x1_p"], nth("x1_p", i, 2 * r + tail - 1))
                h = 64 * (r // 4)
                if tail:
                    act.activation(pjt[h:h + 64, 1, :], pM[0:64, 0:ROW], ACT.Identity,
                                   bias=bp[0:64, 1:2], scale=1.0 / WSC).then_inc(S["pj_act"], 1)
                else:
                    act.activation(pjt[:, 0, :], pM[:, 0:ROW], ACT.Identity, bias=bp[:, 0:1],
                                   scale=1.0 / WSC).then_inc(S["pj_act"], 1)

            def body(i, prev, att, nxt):
                for p in range(PAIRS):
                    if att:
                        exp(i, p)
                    if p % 2 and (p >= 3 and att or p < 3 and prev):
                        out_hi(i if p >= 3 else i - 1, ((p - 3) % PAIRS) // 2)
                    q = qk_steps(p, att, nxt)
                    if q:
                        qk_hi(i + q[0], q[1], q[2][0])
                    if p >= 1 and att or p < 1 and prev:
                        turned_hi(i if p >= 1 else i - 1, (p - 1) % PAIRS)
                    v = v_step(p, att, nxt)
                    if v:
                        v_hi(i + v[0], v[1])
                    if q:
                        qk_hi(i + q[0], q[1], q[2][1])
                    pj = proj_step(p, prev, att)
                    if pj:
                        project_out(i + pj[0], pj[1], pj[2])
                    b = blur_step(p, 11, prev)
                    if b is not None:
                        act.wait_ge(S["xcf_p"], nth("xcf_p", i - 1, b + 1))
                        if b >= 2:
                            act.wait_ge(S["c1_pe"], nth("c1_pe", i - 1, b - 1))
                        act.copy(xc[:, b % 2, 0, :], xcf[0:SY, b % 2, :]).then_inc(S["xch_a"], 1)
                    b = blur_step(p, 13, prev)
                    if b is not None:
                        act.wait_ge(S["c1_pe"], nth("c1_pe", i - 1, b + 1))
                        if b >= 2:
                            act.wait_ge(S["c2_pe"], nth("c2_pe", i - 1, b - 1))
                        act.activation(z[:, b % 2, 0, :], pM[0:SY, 0:3 * SY], ACT.Copy,
                                       scale=1.0 / ASC).then_inc(S["z_act"], 1)
                    n = norm_step(p, att, nxt)
                    if n:
                        norm_hi(i + n[0], n[1], n[2])

            bodies(act, body)

        @block.vector
        def _(dve):
            count = [0]

            def then(ins):
                count[0] += 1
                ins.then_inc(S["setup"], 1)
                dve.wait_ge(S["setup"], count[0])

            then(dve.memset(tabs[:, 1, :], 0.0))
            dve.wait_ge(S["const_in"], 13 * 16)
            ri = xm[:, 1, 0:NT * NT].bitcast(I32)
            then(dve.tensor_scalar(hot[0][:, 0:NT * NT], ri, const("iota")[:, 0:1], None, ALU.is_equal))
            then(dve.tensor_scalar(hot[1][:, 0:NT * NT], ri, const("iota")[:, 1:2], None, ALU.is_equal))
            then(dve.tensor_copy(tabh[:, 0, :, :], tabs))
            then(dve.tensor_tensor(tabh[:, 1, :, :], tabs, tabh[:, 0, :, :], ALU.subtract))
            assert count[0] == SET_HOT, count
            then(dve.memset(mhalf[:, :], -0.5))
            wf = xm[:, 0, 0:8 * C]
            then(dve.tensor_scalar(wf, wf, WSC, None, ALU.mult))
            then(dve.tensor_copy(wmh[:, :], wf[:, 0:4 * C]))
            then(dve.tensor_copy(wth[:, :], wf[:, 4 * C:8 * C]))
            then(dve.tensor_tensor(wml[:, :], wf[:, 0:4 * C], wmh[:, :], ALU.subtract))
            then(dve.tensor_tensor(wtl[:, :], wf[:, 4 * C:8 * C], wth[:, :], ALU.subtract))
            then(dve.memset(vv[:, :, :, :, :, :], 0.0))
            for b in (0, 1):
                then(dve.memset(qst[:, b, NHP * CHUNK:NHP * CHUNK + QPAD], 0.0))
            off, rnd, sub = (xt[0:SY, 0, 2 * POS * n:2 * POS * (n + 1)] for n in (0, 1, 2))
            then(dve.tensor_scalar(off, off, FAR, -FAR, ALU.min, ALU.max))
            then(dve.tensor_scalar(rnd, off, ROUND, None, ALU.add))
            then(dve.tensor_scalar(rnd, rnd, ROUND, None, ALU.subtract))
            then(dve.tensor_tensor(sub, off, rnd, ALU.subtract))
            u0 = const("u0", SY).rearrange("p (o y) -> p o y", o=1).to_broadcast([SY, 2 * POS, HW])
            then(dve.tensor_tensor(dist, u0, spread(rnd, HW), ALU.add))
            then(dve.tensor_tensor(gauss, dist, spread(sub, HW), ALU.add))
            then(dve.tensor_tensor(gauss, gauss, gauss, ALU.mult))
            tp = const("taps", SY).rearrange("p (o t) -> p o t", o=1).to_broadcast([SY, 2 * POS, TAPS])
            then(dve.tensor_tensor(tapv, tp, spread(sub, TAPS), ALU.add))
            then(dve.tensor_tensor(tapv, tapv, tapv, ALU.mult))
            assert count[0] == SET_GAUSS, count
            then(dve.tensor_tensor(dist, dist, dist, ALU.mult))
            then(dve.tensor_scalar(dist, dist, (TAPS // 2 + 0.5) ** 2, None, ALU.is_le))
            inside, upper = (xt[0:SY, 0, 2 * POS * n:2 * POS * (n + 1)] for n in (3, 4))
            then(dve.tensor_scalar(inside, rnd, const("ys", SY), -0.5, ALU.add, ALU.is_ge))
            then(dve.tensor_scalar(upper, rnd, const("ys", SY), HW - 0.5, ALU.add, ALU.is_le))
            then(dve.tensor_tensor(inside, inside, upper, ALU.mult))
            dve.wait_ge(S["setup_act"], 2)
            then(dve.tensor_reduce(upper, tapv, AX.X, ALU.add))
            then(dve.reciprocal(upper, upper))
            then(dve.scalar_tensor_tensor(out=inside, in0=upper, scalar=ASC, in1=inside, op0=ALU.mult, op1=ALU.mult))
            then(dve.tensor_tensor(gauss, gauss, dist, ALU.mult))
            then(dve.tensor_tensor(gauss, gauss, spread(inside, HW), ALU.mult))
            for s in (0, 1):
                v = slice(HW * s, HW * s + HW)
                m = const("smask", SY)[:, s:s + 1]
                then(dve.tensor_scalar(amat[:, 0, :, v], gauss, m, None, ALU.mult))
                then(dve.scalar_tensor_tensor(out=amat[:, 1, :, v], in0=gauss, scalar=m,
                                              in1=amat[:, 0, :, v], op0=ALU.mult, op1=ALU.subtract))
            then(dve.memset(biasT[:, :], 0.0))
            dve.wait_ge(S["setup_pe"], 1)
            bt = heads(biasT[:, :])
            for row, bank in ((0, pT_), (64, pS)):
                for half, j0, j1 in ((0, 0, 42), (1, 42, NT)):
                    src = hot_out(bank)[0:NT, half, 0:NH * (j1 - j0)].rearrange("p (j h) -> p h j", h=NH)
                    then(dve.tensor_copy(bt[row:row + NT, :, j0:j1], src))
            assert count[0] == SET_ALL, count

            def norm(i, c, s):
                row, tail = 2 * c + s % 2, s // 2
                dve.wait_ge(S["gn1_pool"], nth("gn1_pool", i, 1))
                done = 4 * c + s - 1
                if due("xnh_a", i, done):
                    dve.wait_ge(S["xnh_a"], nth("xnh_a", i, done))
                if tail:
                    dve.wait_ge(S["xnl_p"], nth("xnl_p", i, 2 * c + s - 1))
                o = wmajor(xnf[0:64 if tail else 128, s % 2, :])
                if tail:
                    h, t = 64 * (row // 4), slice(ROW * (row % 4), ROW * (row % 4) + ROW)
                    src, g = windows(xt[h:h + 64, par(i), t]), slice(h, h + 64)
                else:
                    src, g = windows(xm[:, par(i), ROW * row:ROW * row + ROW]), slice(0, 128)
                dve.tensor_scalar(o, src, gmean[0][g, tail:tail + 1], grs[0][g, tail:tail + 1],
                                  ALU.subtract, ALU.mult).then_inc(S["xnf_d"], 1)
                if tail:
                    dve.wait_ge(S["xnh_a"], nth("xnh_a", i, 4 * c + s + 1))
                    t = slice(ROW * (row % 4), ROW * (row % 4) + ROW)
                    dve.tensor_tensor(xnt[64:128, t], xnf[0:64, s % 2, :], xnt[0:64, t],
                                      ALU.subtract).then_inc(S["xtl_d"], 1)

            def qk_lo(i, c, g):
                dve.wait_ge(S["qk_act"], nth("qk_act", i, 6 * c + g + 1))
                blk, t, ps = g // 2, slice(ROW * (g % 2), ROW * (g % 2) + ROW), pQ[:, 0:ROW]
                qs = HD ** -0.5 / WSC

                def low(o, hi, rows, scale):
                    return dve.scalar_tensor_tensor(out=o, in0=ps[rows], scalar=scale, in1=hi,
                                                    op0=ALU.mult, op1=ALU.subtract)
                a, k = slice(0, 128), const("kmask")
                if blk == 0:
                    last = low(qks[:, 1, t], qks[:, 0, t], a, qs)
                elif blk == 1:
                    for odd in (0, 1):
                        last = low(qks[:, 4 + odd, t], qks[:, 2 + odd, t], a, k[:, odd:odd + 1])
                else:
                    low(mix[0:64, 1, t], mix[0:64, 0, t], slice(0, 64), qs)
                    a = slice(64, 128)
                    for odd in (0, 1):
                        last = low(mix[a, 2 + odd, t], mix[a, odd, t], a, k[a, odd:odd + 1])
                last.then_inc(S["qk_dve"], 1)

            def v_lo(i, step):
                dve.wait_ge(S["v_act"], nth("v_act", i, step + 1))
                dve.scalar_tensor_tensor(out=v_out(step, 1), in0=pairs2(pV[0:98, 0:2 * C]), scalar=1.0 / WSC,
                                         in1=v_out(step, 0), op0=ALU.mult,
                                         op1=ALU.subtract).then_inc(S["v_dve"], 1)

            def s_view():
                return pS[:, :, 0:294].rearrange("p b (h j) -> p b h j", j=NT)

            def maximum(i, p):
                dve.wait_ge(S["s_pe"], nth("s_pe", i, p + 1))
                dve.tensor_reduce(mx[:, p % 2, :].rearrange("p (b h) -> p b h", b=2), s_view(), AX.X,
                                  ALU.max).then_inc(S["max_d"], 1)

            def subtract(i, p):
                dve.wait_ge(S["max_d"], nth("max_d", i, p + 1))
                if due("norm_p", i, p - 1):
                    dve.wait_ge(S["norm_p"], nth("norm_p", i, p - 1))
                m = mx[:, p % 2, :].rearrange("p (b h o) -> p b h o", b=2, o=1).to_broadcast([128, 2, 6, NT])
                dve.tensor_tensor(prob[:, p % 2, :].rearrange("p (b h j) -> p b h j", b=2, j=NT), s_view(),
                                  m, ALU.subtract).then_inc(S["sub_d"], 1)

            def denominators(i, p):
                dve.wait_ge(S["exp_a"], nth("exp_a", i, p + 1))
                dve.tensor_reduce(den[:, p % 2, :], heads(prob[:, p % 2, :]), AX.X,
                                  ALU.add).then_inc(S["sum_d"], 1)

            def inverse(i, p):
                dve.wait_ge(S["sum_d"], nth("sum_d", i, p + 1))
                dve.reciprocal(den[:, p % 2, :], den[:, p % 2, :]).then_inc(S["rden_d"], 1)

            def turned_lo(i, p):
                dve.wait_ge(S["t_act"], nth("t_act", i, p + 1))
                dve.scalar_tensor_tensor(out=pT[0:98, p % 2, 1], in0=turned(), scalar=PSC,
                                         in1=pT[0:98, p % 2, 0], op0=ALU.mult,
                                         op1=ALU.subtract).then_inc(S["t_dve"], 1)

            def out_lo(i, k):
                dve.wait_ge(S["o_act"], nth("o_act", i, k + 1))
                r, t = k // 2, slice(196 * (k % 2), 196 * (k % 2) + 196)
                dve.scalar_tensor_tensor(out=pairs2(om[:, r % 2, 1, t]), in0=pO[:, :, 0, 0:98], scalar=1.0 / PSC,
                                         in1=pairs2(om[:, r % 2, 0, t]), op0=ALU.mult, op1=ALU.subtract)
                dve.scalar_tensor_tensor(out=pairs2(ot[64:128, r % 2, t]), in0=pO[0:64, :, 1, 0:98],
                                         scalar=1.0 / PSC, in1=pairs2(ot[0:64, r % 2, t]), op0=ALU.mult,
                                         op1=ALU.subtract).then_inc(S["o_dve"], 1)

            def aggregate(n, i):
                name = f"gn{n + 1}_dve"
                dve.bn_aggr(gmv[n][:, 0, :], gst[n][:, 0:8, :]).then_inc(S[name], 1)
                dve.bn_aggr(gmv[n][:, 1, :], gst[n][:, 8:12, :]).then_inc(S[name], 1)

            def center(n, i, ps):
                name = f"gn{n + 1}_dve"
                dve.wait_ge(S[f"gn{n + 1}_pe"], nth(f"gn{n + 1}_pe", i, 1))
                dve.tensor_copy(gmean[n][:, :], ps[:, 0:2]).then_inc(S[name], 1)
                dve.wait_ge(S[name], nth(name, i, 3))
                dve.tensor_tensor(gd[n][:, :], gmv[n][:, :, 0], gmean[n][:, :], ALU.subtract).then_inc(S[name], 1)
                dve.wait_ge(S[name], nth(name, i, 4))
                dve.tensor_tensor(gd[n][:, :], gd[n][:, :], gd[n][:, :], ALU.mult).then_inc(S[name], 1)
                dve.wait_ge(S[name], nth(name, i, 5))
                dve.tensor_tensor(gv[n][:, :], gd[n][:, :], gmv[n][:, :, 1], ALU.add).then_inc(S[name], 1)

            def add_eps(n, i, ps):
                dve.wait_ge(S[f"gn{n + 1}_pe"], nth(f"gn{n + 1}_pe", i, 2))
                dve.tensor_scalar(gve[n][:, :], ps[:, 0:2], EPS, None, ALU.add).then_inc(S[f"gn{n + 1}_dve"], 1)

            def body(i, prev, att, nxt):
                for p in range(PAIRS):
                    if prev and p == 7:
                        dve.wait_ge(S["gn2_bn"], nth("gn2_bn", i - 1, 12))
                    if nxt and p == 17:
                        dve.wait_ge(S["gn1_bn"], nth("gn1_bn", i + 1, 12))
                    if att:
                        maximum(i, p)
                        subtract(i, p)
                    if prev and p == 7:
                        aggregate(1, i - 1)
                    if nxt and p == 17:
                        aggregate(0, i + 1)
                    if p % 2 and (p >= 3 and att or p < 3 and prev):
                        out_lo(i if p >= 3 else i - 1, ((p - 3) % PAIRS) // 2)
                    if att:
                        denominators(i, p)
                        inverse(i, p)
                    q = qk_steps(p, att, nxt)
                    if q:
                        qk_lo(i + q[0], q[1], q[2][0])
                    for r in range(NWX):
                        if p == PPR * r + 9 and att:
                            dve.wait_ge(S["x1_p"], nth("x1_p", i, 2 * r + 1))
                        if p == PPR * r + 9 - PAIRS and prev:
                            dve.wait_ge(S["x1_p"], nth("x1_p", i - 1, 2 * r + 1))
                    if prev and p == 6:
                        dve.wait_ge(S["x1_p"], nth("x1_p", i - 1, 16))
                    if nxt and p == 11:
                        dve.wait_ge(S["x_in"], nth("x_in", i + 1, 48))
                    if p >= 1 and att or p < 1 and prev:
                        turned_lo(i if p >= 1 else i - 1, (p - 1) % PAIRS)
                    v = v_step(p, att, nxt)
                    if v:
                        v_lo(i + v[0], v[1])
                    if q:
                        qk_lo(i + q[0], q[1], q[2][1])
                    for r in range(NWX):
                        s = PPR * r + 9
                        if s == p and att or s - PAIRS == p and prev:
                            im = i if s == p else i - 1
                            dve.bn_stats(gst[1][:, r, :], xm[:, par(im), ROW * r:ROW * r + ROW]).then_inc(S["gn2_bn"], 1)
                    if prev and p == 6:
                        for t in range(4):
                            dve.bn_stats(gst[1][:, 8 + t, :],
                                         xt[:, par(i - 1), ROW * t:ROW * t + ROW]).then_inc(S["gn2_bn"], 1)
                    if prev and p == 7:
                        center(1, i - 1, pM)
                    if prev and p == 8:
                        add_eps(1, i - 1, pM)
                    if prev and p == 9:
                        dve.wait_ge(S["gn2_pool"], nth("gn2_pool", i - 1, 1))
                        dve.scalar_tensor_tensor(out=gnb[:, :], in0=gmean[1][:, :], scalar=-1.0, in1=grs[1][:, :],
                                                 op0=ALU.mult, op1=ALU.mult).then_inc(S["gn2_dve"], 1)
                        dve.wait_ge(S["gn2_dve"], nth("gn2_dve", i - 1, 8))
                        if due("xcl_p", i - 1, 0):
                            dve.wait_ge(S["xcl_p"], nth("xcl_p", i - 1, 0))
                        for n, g in enumerate((grs[1], gnb)):
                            dve.tensor_scalar(cmain[:, n, :], const("sm"), g[:, 0:1], None,
                                              ALU.mult).then_inc(S["gn2_dve"], 1)
                            dve.tensor_scalar(ctail[:, n, :], const("sm", CT)[:, 0:CT // 2], g[0:64, 1:2], None,
                                              ALU.mult).then_inc(S["gn2_dve"], 1)
                    if prev and p == 10:
                        dve.wait_ge(S["gn2_pe"], nth("gn2_pe", i - 1, 3))
                        dve.tensor_copy(coef[:, :, :], pM[0:SY, 0:2 * CC].rearrange("p (a c) -> p a c", a=2)
                                        ).then_inc(S["gn2_dve"], 1)
                    b = blur_step(p, 13, prev)
                    if b is not None:
                        dve.wait_ge(S["z_act"], nth("z_act", i - 1, b + 1))
                        dve.scalar_tensor_tensor(out=z[:, b % 2, 1, :], in0=pM[0:SY, 0:3 * SY], scalar=1.0 / ASC,
                                                 in1=z[:, b % 2, 0, :], op0=ALU.mult,
                                                 op1=ALU.subtract).then_inc(S["z_dve"], 1)
                    b = blur_step(p, 14, prev)
                    if b is not None:
                        dve.wait_ge(S["c2_pe"], nth("c2_pe", i - 1, b + 1))
                        y = xr[:, BC * HW * b:BC * HW * (b + 1)]
                        dve.scalar_tensor_tensor(out=y, in0=pM[0:SY, 0:3 * SY], scalar=1.0 / ASC, in1=y,
                                                 op0=ALU.mult, op1=ALU.add).then_inc(S["y_dve"], 1)
                    if nxt and 11 <= p < 17:
                        for r in (2 * (p - 11), 2 * (p - 11) + 1):
                            src = xm[:, par(i + 1), ROW * r:ROW * r + ROW] if r < 8 else \
                                xt[:, par(i + 1), ROW * (r - 8):ROW * (r - 7)]
                            dve.bn_stats(gst[0][:, r, :], src).then_inc(S["gn1_bn"], 1)
                    if nxt and p == 17:
                        center(0, i + 1, pQ)
                    if nxt and p == 18:
                        add_eps(0, i + 1, pQ)
                    n = norm_step(p, att, nxt)
                    if n:
                        norm(i + n[0], n[1], n[2])

            bodies(dve, body)

        @block.gpsimd
        def _(pool):
            pool.wait_ge(S["setup"], SET_ALL)

            def norm_lo(i, c, s):
                row = 2 * c + s
                pool.wait_ge(S["xnh_a"], nth("xnh_a", i, 4 * c + s + 1))
                t = slice(ROW * (row % 4), ROW * (row % 4) + ROW)
                pool.tensor_tensor(xnl[:, t], xnf[:, s, :], xnh[:, t], ALU.subtract).then_inc(S["xnl_p"], 1)
                pool.wait_ge(S["xnl_p"], nth("xnl_p", i, 2 * c + s + 1))

            def add_residual(i, r, tail):
                pool.wait_ge(S["pj_act"], nth("pj_act", i, 2 * r + tail + 1))
                pool.wait_ge(S["xnf_d"], nth("xnf_d", i, 4 * (r // 2) + 4))
                if tail:
                    h, t = 64 * (r // 4), slice(ROW * (r % 4), ROW * (r % 4) + ROW)
                    v, a = windows(xt[h:h + 64, par(i), t]), wmajor(pjt[h:h + 64, 1, :])
                else:
                    v, a = windows(xm[:, par(i), ROW * r:ROW * r + ROW]), wmajor(pjt[:, 0, :])
                pool.tensor_tensor(v, v, a, ALU.add).then_inc(S["x1_p"], 1)
                pool.wait_ge(S["x1_p"], nth("x1_p", i, 2 * r + tail + 1))

            def body(i, prev, att, nxt):
                for p in range(PAIRS):
                    n = norm_step(p - 1, att, nxt)
                    if n and n[2] < 2:
                        norm_lo(i + n[0], n[1], n[2])
                    pj = proj_step(p - 1, prev, att) if p else ((-1, 6, 0) if prev else None)
                    if pj:
                        add_residual(i + pj[0], pj[1], pj[2])
                    if nxt and p == 19:
                        pool.wait_ge(S["gn1_dve"], nth("gn1_dve", i + 1, 7))
                        if due("xnf_d", i, 16):
                            pool.wait_ge(S["xnf_d"], nth("xnf_d", i, 16))
                        pool.tensor_tensor(grs[0][:, :], gve[0][:, :], mhalf[:, :],
                                           ALU.pow).then_inc(S["gn1_pool"], 1)
                        pool.wait_ge(S["gn1_pool"], nth("gn1_pool", i + 1, 1))
                    if prev and p == 9:
                        pool.wait_ge(S["gn2_dve"], nth("gn2_dve", i - 1, 7))
                        pool.tensor_tensor(grs[1][:, :], gve[1][:, :], mhalf[:, :],
                                           ALU.pow).then_inc(S["gn2_pool"], 1)
                        pool.wait_ge(S["gn2_pool"], nth("gn2_pool", i - 1, 1))
                    b = blur_step(p, 12, prev)
                    if b is not None:
                        pool.wait_ge(S["xch_a"], nth("xch_a", i - 1, b + 1))
                        pool.tensor_tensor(xc[:, b % 2, 1, :], xcf[0:SY, b % 2, :], xc[:, b % 2, 0, :],
                                           ALU.subtract).then_inc(S["xcl_p"], 1)
                        pool.wait_ge(S["xcl_p"], nth("xcl_p", i - 1, b + 1))
                    b = blur_step(p, 11, prev)
                    if b is not None:
                        if b == 0:
                            pool.wait_ge(S["xr_in"], nth("xr_in", i - 1, 32))
                            pool.wait_ge(S["gn2_dve"], nth("gn2_dve", i - 1, 13))
                        cols = slice(BC * b, BC * b + BC)
                        v = xcf[0:SY, b % 2, :].rearrange("p (c x) -> p c x", x=HW)
                        src = xr[:, BC * HW * b:BC * HW * (b + 1)].rearrange("p (c x) -> p c x", x=HW)
                        pool.tensor_tensor(v, src, spread(coef[:, 0, cols], HW), ALU.mult).then_inc(S["xcm_p"], 1)
                        pool.wait_ge(S["xcm_p"], nth("xcm_p", i - 1, b + 1))
                        pool.tensor_tensor(v, v, spread(coef[:, 1, cols], HW), ALU.add).then_inc(S["xcf_p"], 1)
                        pool.wait_ge(S["xcf_p"], nth("xcf_p", i - 1, b + 1))
                    if att:
                        pool.wait_ge(S["rden_d"], nth("rden_d", i, p + 1))
                        if due("t_pe", i, p - 1):
                            pool.wait_ge(S["t_pe"], nth("t_pe", i, p - 1))
                        pool.tensor_tensor(heads(probn[:, p % 2, :]), heads(prob[:, p % 2, :]),
                                           spread(den[:, p % 2, :], NT), ALU.mult).then_inc(S["norm_p"], 1)
                        pool.wait_ge(S["norm_p"], nth("norm_p", i, p + 1))

            bodies(pool, body)


def kernel(x, L0_conv_w_qkv, L0_conv_w_proj, L0_conv_b_proj, L0_conv_bias_table, L0_conv_rel_index,
           L1_conv_offset):
    import concourse.bacc as bacc
    from concourse.bass_utils import run_bass_kernel_spmd as run

    x, wq, wp = (np.asarray(a) for a in (x, L0_conv_w_qkv, L0_conv_w_proj))
    q, k, v = wq[:C].T, wq[C:2 * C].T, wq[2 * C:].T
    v = v.reshape(C, NHP, 2, HD).transpose(0, 2, 3, 1).reshape(C, C)
    w = np.concatenate([q[:, :CM], k[:, :CM], q[:, CM:], k[:, CM:], v, wp.T], 1)
    cf, ch = constants()
    arrays = {"in_x": x, "in_w": np.ascontiguousarray(w),
              "in_b": np.asarray(L0_conv_b_proj).reshape(C, 1), "in_table": np.asarray(L0_conv_bias_table),
              "in_rel": np.asarray(L0_conv_rel_index), "in_offset": np.asarray(L1_conv_offset),
              "in_cf": cf, "in_ch": ch}
    nc = bacc.Bacc("TRN2", target_bir_lowering=False, num_devices=1)
    aps = [nc.dram_tensor(n, a.shape, mybir.dt.from_np(a.dtype), kind="ExternalInput").ap()
           for n, a in arrays.items()]
    scratch = nc.dram_tensor("x1_scratch", (C, TOK), F32, kind="Internal").ap()
    out = nc.dram_tensor("out_0", x.shape, F32, kind="ExternalOutput").ap()
    build(nc, *aps, scratch, out)
    r = run(nc, [arrays], core_ids=[0])
    return r.results[0]["out_0"]
```

```python
from contextlib import ExitStack

import numpy as np
import concourse.bass as bass
from concourse import mybir

F32 = mybir.dt.float32
F16 = mybir.dt.float16
I32 = mybir.dt.int32
ALU = mybir.AluOpType
ACT = mybir.ActivationFunctionType
AX = mybir.AxisListType

C, HW = 192, 56
CM, CT = 128, 64
WS, NH, HD = 7, 12, 16
NT = WS * WS
NWX = HW // WS
ROW = NWX * NT
TOK = HW * HW
CHUNK = 2 * ROW
NCH = TOK // CHUNK
PAIRS = NWX * NWX // 2
PPC = PAIRS // NCH
PPR = NWX // 2
NHP = NH // 2
DH = 4
DC = DH * NT
QPAD = 16
POS, CPP = 8, C // 8
CC = C // 2
BC = 6
NB = CC // BC
SY = 2 * HW
WSC = 256.0
PSC = 1024.0
ASC = 64.0
GROUPS = 32
CPG = C // GROUPS
EPS = 1e-5
TAPS, SIGMA = 5, 0.5
ROUND = 1.5 * 2.0 ** 23
FAR = 2.0 ** 20
NREL = (2 * WS - 1) ** 2
LATE_TAIL = 3
EARLY = 6

CF = {}
_at = 0
for _n, _w in (("ident", 128), ("gmm", 128), ("gtm", 128), ("gmt", 128), ("gtt", 128), ("lm", SY),
               ("sm", CM // 2), ("kmask", 2), ("tscale", 1), ("u0", HW), ("ys", 1), ("smask", 2),
               ("taps", TAPS), ("iota", 2)):
    CF[_n] = (_at, _at + _w)
    _at += _w
NCF = _at
KEEP = CF["u0"][0]


def constants():
    f = np.zeros((128, NCF), np.float32)
    p = np.arange(128)

    def put(name, a):
        f[:a.shape[0], CF[name][0]:CF[name][1]] = a

    put("ident", np.eye(128))
    gm, gt = p // CPG, (CM + p % CT) // CPG
    put("gmm", (gm[:, None] == gm[None]) / CPG)
    put("gtm", (gt[:, None] == gm[None]) / (2 * CPG))
    put("gmt", (gm[:, None] == gt[None]) / CPG)
    put("gtt", (gt[:, None] == gt[None]) / (2 * CPG))
    put("lm", p[:, None] % 2 == np.arange(SY)[None] // HW)
    put("sm", p[:, None] // 2 == np.arange(CM // 2)[None])
    put("kmask", np.stack([p // HD % 2 == 0, p // HD % 2 == 1], 1) / WSC)
    put("tscale", np.where(p < 64, -HD ** -0.5, p // HD % 2 == 0)[:, None] / WSC)
    put("u0", (p[:SY, None] % HW) - np.arange(HW)[None])
    put("ys", p[:SY, None] % HW)
    put("smask", np.stack([p < HW, (p >= HW) & (p < SY)], 1)[:SY])
    put("taps", np.tile(np.arange(TAPS) - TAPS // 2, (128, 1)))
    put("iota", np.stack([p, p + 128], 1))
    h = np.zeros((128, 128), np.float16)
    h[(p[:, None] % 64 == p[None] % 64) & (p[:, None] % 64 < NT)] = -1
    return f, h


class Image:

    def __init__(self, base, shift=0):
        self.base, self.shift = base, shift

    def __add__(self, n):
        return Image(self.base, self.shift + n)

    def __sub__(self, n):
        return self + -n

    def row(self):
        return self.base + self.shift


SET_HOT, SET_GAUSS, SET_ALL = 5, 23, 42


def build(nc, x, w_in, b_out, table, rel, offset, cf, ch, scratch, out):
    images = x.shape[0]
    ctx = ExitStack()
    with ctx:
        def sb(name, shape, dt):
            return ctx.enter_context(nc.sbuf_tensor(name, shape, dt))

        def pb(name, shape):
            return ctx.enter_context(nc.psum_tensor(name, shape, F32))

        def sem(name):
            return ctx.enter_context(nc.semaphore(name))

        xm = sb("xm", [128, 2, TOK], F32)
        xt = sb("xt", [128, 2, TOK // 2], F32)
        xnh = sb("xnh", [128, 2 * CHUNK], F16)
        xnl = sb("xnl", [128, 2 * CHUNK], F16)
        xnt = sb("xnt", [128, 2 * CHUNK], F16)
        xnf = sb("xnf", [128, 2, ROW], F32)
        qks = sb("qks", [128, 6, CHUNK], F16)
        mix = sb("mix", [128, 4, CHUNK], F16)
        kst = sb("kst", [96, 2, NHP, 2, CHUNK], F16)
        qst = sb("qst", [96, 2, NHP * CHUNK + QPAD], F16)
        prob = sb("prob", [128, 2, NH * NT], F32)
        probn = sb("probn", [128, 2, NH * NT], F32)
        pT = sb("pT", [128, 2, 2, NH, NT], F16)
        cv = sb("cv", [98, 2, PPR, 2, C], F16)
        vv = sb("vv", [98, 2, 2, PPR, 2, C], F16)
        om = sb("om", [128, 2, 2, ROW], F16)
        ot = sb("ot", [128, 2, ROW], F16)
        pjt = sb("pjt", [128, 2, ROW], F32)
        wmh = sb("wmh", [128, 4 * C], F16)
        wml = sb("wml", [128, 4 * C], F16)
        wth = sb("wth", [128, 4 * C], F16)
        wtl = sb("wtl", [128, 4 * C], F16)
        bp = sb("bp", [128, 2], F32)
        biasT = sb("biasT", [128, NH * NT], F16)
        xr = sb("xr", [SY, CC * HW], F32)
        xcf = sb("xcf", [128, 2, BC * HW], F32)
        xc = sb("xc", [SY, 2, 2, BC * HW], F16)
        z = sb("z", [SY, 2, 2, 3 * SY], F16)
        amat = sb("amat", [SY, 2, 2 * POS, SY], F16)
        cst = sb("cst", [128, KEEP], F32)
        addb = sb("addb", [128, 128], F16)
        mx = sb("mx", [128, 2, NH], F32)
        den = sb("den", [128, 2, NH], F32)
        gst = [sb(f"gst{n}", [128, 12, 6], F32) for n in (1, 2)]
        gmv = [sb(f"gmv{n}", [128, 2, 2], F32) for n in (1, 2)]
        gmean = [sb(f"gmean{n}", [128, 2], F32) for n in (1, 2)]
        gd = [sb(f"gd{n}", [128, 2], F32) for n in (1, 2)]
        gv = [sb(f"gv{n}", [128, 2], F32) for n in (1, 2)]
        gve = [sb(f"gve{n}", [128, 2], F32) for n in (1, 2)]
        grs = [sb(f"grs{n}", [128, 2], F32) for n in (1, 2)]
        mhalf = sb("mhalf", [128, 2], F32)
        gneg = sb("gneg", [128, 2], F32)
        gbias = sb("gbias", [128, 2], F32)
        gnb = sb("gnb", [128, 2], F32)
        coef = sb("coef", [SY, 2, CC], F32)

        cmain, ctail = (xcf[0:n, b, 0:n].rearrange("p (a c) -> p a c", a=2)
                        for b, n in ((0, CM), (1, CT)))

        def const(name, rows=128):
            a, b = CF[name]
            return cst[0:rows, a:b] if b <= KEEP else cset[0:rows, a - KEEP:b - KEEP]

        pS = pb("pS", [128, 2, 512])
        pT_ = pb("pTr", [128, 1024])
        pO = pb("pO", [128, 2, 2, 128])
        pV = pb("pV", [128, 512])
        pQ = pb("pQ", [128, 512])
        pM = pb("pM", [128, 512])

        S = {n: sem(n) for n in (
            "const_in", "setup", "setup_act", "setup_pe",
            "x_in", "x1_out", "xr_in", "y_out", "stack_q", "stack_k", "stack_t", "v_spread0", "v_spread1",
            "gn1_bn", "gn2_bn", "gn1_dve", "gn1_pe", "gn1_pool", "gn2_dve", "gn2_pe", "gn2_pool",
            "xnh_a", "xnl_p", "xtl_d",
            "qk_pe", "qk_act", "qk_dve", "v_pe", "v_act", "v_dve",
            "s_pe", "max_d", "sub_d", "direct_a", "exp_a", "sum_d", "rden_d", "norm_p",
            "t_pe", "t_act", "t_dve", "o_pe", "o_act", "o_dve",
            "pj_pe", "pj_act", "x1_p", "xcm_p", "xcf_p", "xch_a", "xcl_p",
            "c1_pe", "z_act", "z_dve", "c2_pe", "y_dve")}
        PER = {"x_in": 64, "x1_out": 128, "xr_in": 64, "y_out": 8 * 16, "stack_q": 192 * NCH,
               "stack_k": 192 * NCH, "stack_t": 192 * NCH, "gn1_bn": 12, "gn2_bn": 12, "gn1_dve": 8, "gn1_pe": 2, "gn1_pool": 2,
               "gn2_dve": 13, "gn2_pe": 3, "gn2_pool": 1, "xnh_a": 16, "xnl_p": 8,
               "xtl_d": 8, "qk_pe": 24, "qk_act": 24, "qk_dve": 24, "pj_pe": 16, "pj_act": 16,
               "x1_p": 16, "o_act": 16, "o_dve": 16}
        PER.update(max_d=2 * PAIRS, v_pe=16, v_act=16, v_dve=16, v_spread0=256, v_spread1=256)
        for n in ("s_pe", "sub_d", "direct_a", "exp_a", "sum_d", "rden_d",
                  "norm_p", "t_pe", "t_act", "t_dve", "o_pe"):
            PER[n] = PAIRS
        for n in ("xcm_p", "xcf_p", "xch_a", "xcl_p", "c1_pe", "z_act", "z_dve", "c2_pe", "y_dve"):
            PER[n] = NB

        def nth(name, i, k):
            return i.base * PER[name] + (i.shift * PER[name] + k)

        def due(name, i, k):
            first = i.base if isinstance(i.base, int) else 1
            return (first + i.shift) * PER[name] + k > 0

        def par(i):
            return (i.base + (i.shift + 2)) % 2

        def windows(ap):
            return ap.rearrange("p (yi wx xi) -> p wx yi xi", yi=WS, wx=NWX)

        def wmajor(ap):
            return ap.rearrange("p (wx yi xi) -> p wx yi xi", yi=WS, wx=NWX)

        def heads(ap):
            return ap.rearrange("p (h j) -> p h j", j=NT)

        def spread(ap, n):
            return ap.rearrange("p (a o) -> p a o", o=1).to_broadcast([ap.shape[0], ap.shape[1], n])

        def norm_step(p, att, nxt):
            for lo, shift, c, on in ((3, 0, 2, att), (11, 0, 3, att), (19, 1, 0, nxt), (27, 1, 1, nxt)):
                if on and lo <= p < lo + 4:
                    return shift, c, p - lo
            return None

        def qk_step(p, att, nxt):
            c, k = divmod(p + 1, PPC)
            shift, cn = divmod(c + 1, NCH)
            if k < 6 and (nxt if shift else att):
                return shift, cn, k
            return None

        def v_step(p, att, nxt):
            if p % 2 and (att if p + 3 < PAIRS else nxt):
                return (p + 3) // PAIRS, (p + 3) % PAIRS // 2
            return None

        def v_out(step, part):
            k = 2 * (step % 2)
            return cv[:, step // 2 % 2, k:k + 2, part, :]

        def proj_step(p, prev, att):
            found = []
            for r in range(NWX):
                for tail in (0, 1):
                    s = PPR * r + 6 + (LATE_TAIL if tail and r % 2 and r < NWX - 1 else 0)
                    if s == p and att:
                        found.append((0, r, tail))
                    if s - PAIRS == p and prev:
                        found.append((-1, r, tail))
            return found

        def before(step, p, prev, att, nxt):
            args = (prev, att) if step is proj_step else (att, nxt)
            if p:
                return step(p - 1, *args)
            args = (True, prev) if step is proj_step else (prev, att)
            last = step(PAIRS - 1, *args)
            if step is proj_step:
                return [(n - 1, *rest) for n, *rest in last]
            return (last[0] - 1, *last[1:]) if last else None

        def tail_bank(r):
            return pM if r == NWX - 1 else pQ

        def blur_step(p, first, prev):
            return p - first if prev and 0 <= p - first < NB else None

        cset = probn[:, 1, 0:NCF - KEEP]
        tabs = probn[:, 0, 0:2 * NH].rearrange("p (a h) -> p a h", a=2)
        tabh = probn[:, 0, 2 * NH:4 * NH].bitcast(F16).rearrange("p (b a h) -> p b a h", a=2, b=2)
        hot = [b[:, :, :].rearrange("p a t -> p (a t)") for b in (qks, mix)]
        dist = xr[:, 0:2 * POS * HW].rearrange("p (a y) -> p a y", y=HW)
        gauss = xr[:, 2 * POS * HW:4 * POS * HW].rearrange("p (a y) -> p a y", y=HW)
        tapv = xr[:, 4 * POS * HW:4 * POS * HW + 2 * POS * TAPS].rearrange("p (a t) -> p a t", t=TAPS)

        def hot_out(bank):
            return bank[:, :, :] if bank is pS else bank[:, :].rearrange("p (b c) -> p b c", b=2)

        def turned():
            return pT_[0:2 * NT, 0:128 * NHP].rearrange("p (q s) -> p q s", s=64)[:, :, 0:NT]

        def pairs2(ap):
            return ap.rearrange("p (a t) -> p a t", a=2)

        block = ctx.enter_context(nc.Block())

        def bodies(eng, body):
            body(Image(-1), False, False, True)
            body(Image(0), False, True, True)
            if images > 2:
                with eng.Fori(1, images - 1) as i:
                    body(Image(i), True, True, True)
            body(Image(images - 1), True, True, False)
            body(Image(images), True, False, False)

        @block.sync
        def _(sp):
            sp.dma_start(cst[:, :], cf[:, 0:KEEP]).then_inc(S["const_in"], 16)
            sp.dma_start(cset, cf[:, KEEP:NCF]).then_inc(S["const_in"], 16)
            sp.dma_start(addb[:, :], ch).then_inc(S["const_in"], 16)
            sp.dma_start(xm[:, 0, 0:4 * C], w_in[0:CM, :]).then_inc(S["const_in"], 16)
            sp.dma_start(xm[0:64, 0, 4 * C:8 * C], w_in[CM:C, :]).then_inc(S["const_in"], 16)
            sp.dma_start(xm[64:128, 0, 4 * C:8 * C], w_in[CM:C, :]).then_inc(S["const_in"], 16)
            sp.dma_start(bp[:, 0:1], b_out[0:CM, :]).then_inc(S["const_in"], 16)
            sp.dma_start(bp[0:64, 1:2], b_out[CM:C, :]).then_inc(S["const_in"], 16)
            sp.dma_start(bp[64:128, 1:2], b_out[CM:C, :]).then_inc(S["const_in"], 16)
            sp.dma_start(tabs[:, 0, :], table[0:128, :]).then_inc(S["const_in"], 16)
            sp.wait_ge(S["setup"], 1)
            sp.dma_start(tabs[0:NREL - 128, 1, :], table[128:NREL, :]).then_inc(S["const_in"], 16)
            sp.dma_start(xm[:, 1, 0:NT * NT].bitcast(I32),
                         rel.rearrange("(o i) j -> o (i j)", o=1).to_broadcast([128, NT * NT])).then_inc(S["const_in"], 16)
            sp.dma_start(xt[0:SY, 0, 0:2 * POS], offset.rearrange("(o q) a -> o (q a)", o=1)
                         .to_broadcast([SY, 2 * POS])).then_inc(S["const_in"], 16)

            def stack(i, c, blk):
                buf, done = c % 2, S[("stack_q", "stack_k", "stack_t")[blk]]
                sp.wait_ge(S["qk_dve"], nth("qk_dve", i, 6 * c + 2 * blk + 2))
                if blk != 1:
                    src = qks if blk == 0 else mix
                    for n, hp in enumerate(range(4) if blk == 0 else range(4, NHP)):
                        for r, part in enumerate((0, 1, 0) if blk == 0 else (0, 2, 0)):
                            sp.dma_start(qst[32 * r:32 * r + 32, buf, CHUNK * hp:CHUNK * hp + CHUNK],
                                         src[32 * n:32 * n + 32, part, :]).then_inc(done, 16)
                if blk != 0:
                    src, row, at = (qks, 0, 2) if blk == 1 else (mix, 64, 0)
                    for n, hp in enumerate(range(4) if blk == 1 else range(4, NHP)):
                        for r, part in enumerate((0, 0, 1)):
                            sp.dma_start(kst[32 * r:32 * r + 32, buf, hp, :, :],
                                         src[row + 32 * n:row + 32 * n + 32,
                                             at + 2 * part:at + 2 * part + 2, :]).then_inc(done, 16)

            def spread_v(i, g):
                sp.wait_ge(S["v_dve"], nth("v_dve", i, 2 * g + 2))
                for w in (0, 1):
                    for a in (0, 1):
                        h = slice(C // 2 * a, C // 2 * a + C // 2)
                        src = cv[NT * w:NT * w + NT, g % 2, :, :, h].rearrange("j p b c -> j (p b) c")
                        dst = vv[NT * a:NT * a + NT, g % 2, w, :, :, h].rearrange("j p b c -> j (p b) c")
                        sp.dma_start(dst, src).then_inc(S[f"v_spread{g % 2}"], 16)

            def store_x1(i, k):
                t, h = slice(CHUNK * k, CHUNK * k + CHUNK), k // 2
                sp.wait_ge(S["x1_p"], nth("x1_p", i, 4 * k + 4))
                sp.dma_start(scratch[0:CM, t], xm[:, par(i), t]).then_inc(S["x1_out"], 16)
                if k == EARLY // 2 - 1 and due("y_out", i, 0):
                    sp.wait_ge(S["y_out"], nth("y_out", i, 0))
                sp.dma_start(scratch[CM:C, t], xt[64 * h:64 * h + 64, par(i), CHUNK * (k % 2):CHUNK * (k % 2) + CHUNK]
                             ).then_inc(S["x1_out"], 16)

            def read_x1(y0, y1):
                v = scratch.rearrange("(c s) (y x) -> s y c x", s=2, x=HW)
                for s in (0, 1):
                    sp.dma_start(xr[HW * s + y0:HW * s + y1, :].rearrange("y (c x) -> y c x", x=HW),
                                 v[s][y0:y1]).then_inc(S["xr_in"], 16)

            def body(i, prev, att, nxt):
                for p in range(PAIRS):
                    qk = before(qk_step, p, prev, att, nxt)
                    if qk and qk[2] % 2:
                        stack(i + qk[0], qk[1], qk[2] // 2)
                    v = before(v_step, p, prev, att, nxt) if p % PPR == 0 else None
                    if v:
                        spread_v(i + v[0], v[1] // 2)
                    if p % PPC == PPC - 1 and p > PPC and att:
                        store_x1(i, p // PPC - 1)
                    if p == 4 and prev:
                        store_x1(i - 1, NCH - 1)
                    if p == 1 and prev:
                        sp.wait_ge(S["x1_out"], nth("x1_out", i - 1, EARLY * 16))
                        read_x1(0, EARLY * WS)
                    if p == 5 and prev:
                        sp.wait_ge(S["x1_out"], nth("x1_out", i, 0))
                        read_x1(EARLY * WS, HW)
                    if p in (2, 6) and nxt:
                        taken = EARLY if p == 2 else 12
                        if due("gn2_bn", i - 1, taken):
                            sp.wait_ge(S["gn2_bn"], nth("gn2_bn", i - 1, taken))
                        if not att:
                            sp.wait_ge(S["setup"], SET_ALL)
                        xi = x[(i + 1).row()].rearrange("c y x -> c (y x)")
                        t = slice(0, EARLY * ROW) if p == 2 else slice(EARLY * ROW, TOK)
                        sp.dma_start(xm[:, par(i + 1), t], xi[0:CM, t]).then_inc(S["x_in"], 16)
                        for h in (0, 1) if p == 6 else ():
                            sp.dma_start(xt[64 * h:64 * h + 64, par(i + 1), :],
                                         xi[CM:C, h * (TOK // 2):(h + 1) * (TOK // 2)]).then_inc(S["x_in"], 16)
                    b = blur_step(p, 14, prev)
                    if b is not None and b % 4 == 3:
                        sp.wait_ge(S["y_dve"], nth("y_dve", i - 1, b + 1))
                        c = slice(b // 4 * CPP, b // 4 * CPP + CPP)
                        v = out[(i - 1).row()].rearrange("(c s) y x -> s y c x", s=2)
                        for s in (0, 1):
                            src = xr[HW * s:HW * s + HW, :].rearrange("y (c x) -> y c x", x=HW)
                            sp.dma_start(v[s][:, c], src[:, c]).then_inc(S["y_out"], 16)

            bodies(sp, body)
            sp.wait_ge(S["y_out"], images * PER["y_out"])

        @block.tensor
        def _(pe):
            def three(out_ap, lh, ll, rh, rl, start=True, stop=True):
                pe.matmul(out_ap, lh, rh, start=start, stop=False, skip_group_check=True)
                pe.matmul(out_ap, ll, rh, start=False, stop=False, skip_group_check=True)
                return pe.matmul(out_ap, lh, rl, start=False, stop=stop, skip_group_check=True)

            pe.wait_ge(S["setup"], SET_HOT)
            for part, bank in ((0, pT_), (1, pS)):
                for j in range(NT):
                    o = hot_out(bank)[0:NT, (j // 42), NH * (j % 42):NH * (j % 42) + NH]
                    for half, rows in ((0, 128), (1, NREL - 128)):
                        lhs = hot[half][0:rows, 0:NT * NT].rearrange("p (i j) -> p j i", j=NT)[:, j, :]
                        mm = pe.matmul(o, lhs, tabh[0:rows, part, half, :], start=(half == 0),
                                       stop=(half == 1), skip_group_check=True)
            mm.then_inc(S["setup_pe"], 1)
            pe.wait_ge(S["setup"], SET_ALL)

            def group_sum(n, o, src):
                for col, (a, b) in enumerate((("gmm", "gtm"), ("gmt", "gtt"))):
                    pe.matmul(o[:, col:col + 1], const(a), src[:, 0:1], start=True, stop=False,
                              skip_group_check=True)
                    mm = pe.matmul(o[:, col:col + 1], const(b), src[:, 1:2], start=False, stop=True,
                                   skip_group_check=True)
                return mm

            def qk(i, c, g):
                if due("qk_dve", i, 6 * c + g):
                    pe.wait_ge(S["qk_dve"], nth("qk_dve", i, 6 * c + g))
                row = 2 * c + g % 2
                pe.wait_ge(S["xnh_a"], nth("xnh_a", i, 4 * c + 4))
                pe.wait_ge(S["xnl_p"], nth("xnl_p", i, 2 * c + 2))
                pe.wait_ge(S["xtl_d"], nth("xtl_d", i, 2 * c + 2))
                w, t, o = slice(128 * (g // 2), 128 * (g // 2) + 128), slice(ROW * (row % 4), ROW * (row % 4) + ROW), pQ[:, 0:ROW]
                three(o, wmh[:, w], wml[:, w], xnh[:, t], xnl[:, t], stop=False)
                pe.matmul(o, wth[:, w], xnt[:, t], start=False, stop=False, skip_group_check=True)
                pe.matmul(o, wtl[0:64, w], xnt[0:64, t], start=False, stop=True,
                          skip_group_check=True).then_inc(S["qk_pe"], 1)

            def values(i, step):
                if due("v_dve", i, step):
                    pe.wait_ge(S["v_dve"], nth("v_dve", i, step))
                c = 2 * step // PPC
                pe.wait_ge(S["xnh_a"], nth("xnh_a", i, 4 * c + 4))
                pe.wait_ge(S["xnl_p"], nth("xnl_p", i, 2 * c + 2))
                pe.wait_ge(S["xtl_d"], nth("xtl_d", i, 2 * c + 2))
                w = slice(3 * 128, 3 * 128 + C)
                for k in (0, 1):
                    at = 2 * NT * ((2 * step + k) % (2 * PPC))
                    t, o = slice(at, at + 2 * NT), pV[0:2 * NT, C * k:C * k + C]
                    three(o, xnh[:, t], xnl[:, t], wmh[:, w], wml[:, w], stop=False)
                    pe.matmul(o, xnt[:, t], wth[:, w], start=False, stop=False, skip_group_check=True)
                    mm = pe.matmul(o, xnt[0:64, t], wtl[0:64, w], start=False, stop=True,
                                   skip_group_check=True)
                mm.then_inc(S["v_pe"], 1)

            def scores(i, p):
                c, q = divmod(p, PPC)
                if q == 0:
                    pe.wait_ge(S["stack_q"], nth("stack_q", i, 192 * (c + 1)))
                    pe.wait_ge(S["stack_k"], nth("stack_k", i, 192 * (c + 1)))
                    pe.wait_ge(S["stack_t"], nth("stack_t", i, 192 * (c + 1)))
                if due("direct_a", i, p):
                    pe.wait_ge(S["direct_a"], nth("direct_a", i, p))
                if due("sub_d", i, p):
                    pe.wait_ge(S["sub_d"], nth("sub_d", i, p))
                for bank, h0, h1 in ((0, 0, DH), (1, DH, NH)):
                    pe.matmul(pS[:, bank, 0:NT * (h1 - h0)], addb[:, :], biasT[:, NT * h0:NT * h1],
                              start=True, stop=False, skip_group_check=True)
                    for win in (0, 1):
                        t = NT * (2 * q + win)
                        for hp in range(h0 // 2, h1 // 2):
                            at = NT * (2 * hp - h0)
                            o = pS[64 * win:64 * win + 64, bank, at:at + 2 * NT]
                            mm = pe.matmul(o.rearrange("p (a j) -> p a j", a=2),
                                           qst[:, c % 2, CHUNK * hp + t:CHUNK * hp + t + 64],
                                           kst[:, c % 2, hp, :, t:t + NT], start=False, stop=True,
                                           skip_group_check=True)
                mm.then_inc(S["s_pe"], 1)

            def turn(i, p):
                pe.wait_ge(S["norm_p"], nth("norm_p", i, p + 1))
                if due("t_dve", i, p):
                    pe.wait_ge(S["t_dve"], nth("t_dve", i, p))
                for hp in range(NHP):
                    mm = pe.transpose(pT_[0:98, 128 * hp:128 * hp + 128],
                                      probn[:, p % 2, 98 * hp:98 * hp + 98], const("ident"))
                mm.then_inc(S["t_pe"], 1)

            def attend(i, p):
                pe.wait_ge(S["t_dve"], nth("t_dve", i, p + 1))
                g = p // PPR
                pe.wait_ge(S[f"v_spread{g % 2}"], nth(f"v_spread{g % 2}", i, 64 * (g // 2 + 1)))
                if p % 2 == 0:
                    if due("o_dve", i, p // 2):
                        pe.wait_ge(S["o_dve"], nth("o_dve", i, p // 2))
                for win in (0, 1):
                    for hps in (range(4), range(4, NHP)):
                        for k, (a, b) in enumerate(((0, 0), (1, 0), (0, 1))):
                            for hp in hps:
                                r = 32 * (hp % 4)
                                mm = pe.matmul(pO[r:r + 32, p % 2, hp // 4, NT * win:NT * win + NT],
                                               vv[:, g % 2, win, p % PPR, a, hp::NHP],
                                               pT[0:98, p % 2, b, 2 * hp + win, :],
                                               start=(k == 0), stop=(k == 2), skip_group_check=True)
                mm.then_inc(S["o_pe"], 1)

            def project(i, r, tail):
                if due("pj_act", i, 2 * r):
                    pe.wait_ge(S["pj_act"], nth("pj_act", i, 2 * r))
                pe.wait_ge(S["o_dve"], nth("o_dve", i, 2 * r + 2))
                n = CT if tail else CM
                at = 3 * C + CM * tail
                w, o = slice(at, at + n), (tail_bank(r) if tail else pV)[0:n, 0:ROW]
                three(o, wmh[:, w], wml[:, w], om[:, r % 2, 0, :], om[:, r % 2, 1, :], stop=False)
                pe.matmul(o, wth[:, w], ot[:, r % 2, :], start=False, stop=False, skip_group_check=True)
                pe.matmul(o, wtl[0:64, w], ot[0:64, r % 2, :], start=False, stop=True,
                          skip_group_check=True).then_inc(S["pj_pe"], 1)

            def blur(i, b, stage):
                if stage == 0:
                    pe.wait_ge(S["xcl_p"], nth("xcl_p", i, b + 1))
                    if b == 0:
                        pe.wait_ge(S["gn2_dve"], nth("gn2_dve", i, 13))
                    else:
                        pe.wait_ge(S["y_dve"], nth("y_dve", i, b))
                    src = xc
                else:
                    pe.wait_ge(S["z_dve"], nth("z_dve", i, b + 1))
                    src = z
                m = 2 * (b // (CPP // 2 // BC)) + (1 if stage == 0 else 0)
                for j in range(BC // 2):
                    k = slice(SY * j, SY * j + SY)
                    mm = three(pM[0:SY, k], src[:, b % 2, 0, k], src[:, b % 2, 1, k],
                               amat[:, 0, m, :], amat[:, 1, m, :])
                mm.then_inc(S["c1_pe" if stage == 0 else "c2_pe"], 1)

            def body(i, prev, att, nxt):
                for p in range(PAIRS):
                    was = before(proj_step, p, prev, att, nxt)
                    if p >= 2 and att or p < 2 and prev:
                        attend(i if p >= 2 else i - 1, (p - 2) % PAIRS)
                    b = blur_step(p, 12, prev)
                    if b is not None:
                        blur(i - 1, b, 0)
                    if p >= 1 and att or p < 1 and prev:
                        turn(i if p >= 1 else i - 1, (p - 1) % PAIRS)
                    if nxt and p in (13, 17):
                        pe.wait_ge(S["gn1_dve"], nth("gn1_dve", i + 1, 3 if p == 13 else 7))
                    v = v_step(p, att, nxt)
                    for n, row, tail in was:
                        if v and not tail:
                            pe.wait_ge(S["pj_act"], nth("pj_act", i + n, 2 * row + 1))
                    if v:
                        values(i + v[0], v[1])
                    if att if p < PAIRS - 1 else nxt:
                        scores(i + (p + 1) // PAIRS, (p + 1) % PAIRS)
                    u = before(v_step, p, prev, att, nxt)
                    for n, row, tail in proj_step(p, prev, att):
                        if not tail and u:
                            pe.wait_ge(S["v_dve"], nth("v_dve", i + u[0], u[1] + 1))
                        w, c = divmod(p // PPC + 1, NCH)
                        if tail and row < NWX - 1 and (nxt if w else att):
                            pe.wait_ge(S["qk_dve"], nth("qk_dve", i + w, 6 * c + 6))
                        if tail and row == NWX - 1 and due("y_dve", i - 1, 0):
                            pe.wait_ge(S["y_dve"], nth("y_dve", i - 1, 0))
                        project(i + n, row, tail)
                    q = qk_step(p, att, nxt)
                    for n, row, tail in was:
                        if q and tail and row < NWX - 1:
                            pe.wait_ge(S["pj_act"], nth("pj_act", i + n, 2 * row + 2))
                    if q:
                        qk(i + q[0], q[1], q[2])
                    if b is not None:
                        blur(i - 1, b, 1)
                    if nxt and p in (12, 16):
                        if u:
                            pe.wait_ge(S["v_dve"], nth("v_dve", i + u[0], u[1] + 1))
                        pe.wait_ge(S["gn1_dve"], nth("gn1_dve", i + 1, 2 if p == 12 else 6))
                        group_sum(1, pV, gmv[0][:, :, 0] if p == 12 else gv[0]).then_inc(S["gn1_pe"], 1)
                    if prev and p == 5:
                        pe.wait_ge(S["pj_act"], nth("pj_act", i - 1, 16))
                        pe.wait_ge(S["gn2_dve"], nth("gn2_dve", i - 1, 2))
                        group_sum(2, pM, gmv[1][:, :, 0]).then_inc(S["gn2_pe"], 1)
                    if prev and p == 6:
                        pe.wait_ge(S["gn2_dve"], nth("gn2_dve", i - 1, 6))
                        group_sum(2, pM, gv[1]).then_inc(S["gn2_pe"], 1)
                    if prev and p == 9:
                        pe.wait_ge(S["gn2_dve"], nth("gn2_dve", i - 1, 12))
                        o = pM[0:SY, 0:2 * CC].rearrange("p (a c) -> p a c", a=2)
                        pe.matmul(o[:, :, 0:CM // 2], const("lm"), cmain, start=True, stop=True,
                                  skip_group_check=True)
                        pe.matmul(o[:, :, CM // 2:CC], const("lm", CT), ctail, start=True, stop=True,
                                  skip_group_check=True).then_inc(S["gn2_pe"], 1)


            bodies(pe, body)

        @block.scalar
        def _(act):
            act.wait_ge(S["setup"], SET_GAUSS)
            act.activation(gauss, gauss, ACT.Exp, scale=-1.0 / (2 * SIGMA ** 2)).then_inc(S["setup_act"], 1)
            act.activation(tapv, tapv, ACT.Exp, scale=-1.0 / (2 * SIGMA ** 2)).then_inc(S["setup_act"], 1)
            act.wait_ge(S["setup"], SET_ALL)

            def norm(i, c, s):
                row, tail = 2 * c + s % 2, s // 2
                act.wait_ge(S["gn1_pool"], nth("gn1_pool", i, 2))
                done = PPC // 2 * (c - 1) - (0 if s % 2 else 2)
                if due("v_pe", i, done):
                    act.wait_ge(S["v_pe"], nth("v_pe", i, done))
                if due("qk_pe", i, 6 * (c - 1)):
                    act.wait_ge(S["qk_pe"], nth("qk_pe", i, 6 * (c - 1)))
                if tail:
                    act.wait_ge(S["xnl_p"], nth("xnl_p", i, 2 * c + s - 1))
                elif due("xtl_d", i, 2 * c + s - 1):
                    act.wait_ge(S["xtl_d"], nth("xtl_d", i, 2 * c + s - 1))
                t = slice(ROW * (row % 4), ROW * (row % 4) + ROW)
                if tail:
                    h, u = 64 * (row // 4), slice(ROW * (row % 4), ROW * (row % 4) + ROW)
                    src, g = windows(xt[h:h + 64, par(i), u]), slice(h, h + 64)
                    hi, full = xnt[0:64, t], xnf[0:64, s % 2, :]
                else:
                    src, g = windows(xm[:, par(i), ROW * row:ROW * row + ROW]), slice(0, 128)
                    hi, full = xnh[:, t], xnf[:, s % 2, :]
                for o in (full, hi):
                    a = act.activation(wmajor(o), src, ACT.Identity, bias=gbias[g, tail:tail + 1],
                                       scale=grs[0][g, tail:tail + 1])
                a.then_inc(S["xnh_a"], 1)

            def qk_hi(i, c, g):
                act.wait_ge(S["qk_pe"], nth("qk_pe", i, 6 * c + g + 1))
                if g == 0 and due("stack_q", i, 192 * c):
                    act.wait_ge(S["stack_q"], nth("stack_q", i, 192 * c))
                if g == 2 and due("stack_k", i, 192 * c):
                    act.wait_ge(S["stack_k"], nth("stack_k", i, 192 * c))
                if g == 4 and due("stack_t", i, 192 * c):
                    act.wait_ge(S["stack_t"], nth("stack_t", i, 192 * c))
                blk, t = g // 2, slice(ROW * (g % 2), ROW * (g % 2) + ROW)
                qs = -HD ** -0.5 / WSC
                if blk == 0:
                    act.activation(qks[:, 0, t], pQ[:, 0:ROW], ACT.Copy, scale=qs).then_inc(S["qk_act"], 1)
                elif blk == 1:
                    act.activation(qks[:, 2, t], pQ[:, 0:ROW], ACT.Copy, scale=const("kmask")[:, 0:1])
                    act.activation(qks[:, 3, t], pQ[:, 0:ROW], ACT.Copy,
                                   scale=const("kmask")[:, 1:2]).then_inc(S["qk_act"], 1)
                else:
                    act.activation(mix[:, 0, t], pQ[:, 0:ROW], ACT.Copy, scale=const("tscale"))
                    act.activation(mix[64:128, 1, t], pQ[64:128, 0:ROW], ACT.Copy,
                                   scale=const("kmask")[64:128, 1:2]).then_inc(S["qk_act"], 1)

            def v_hi(i, step):
                act.wait_ge(S["v_pe"], nth("v_pe", i, step + 1))
                g = step // 2
                if due(f"v_spread{g % 2}", i, 64 * (g // 2)):
                    act.wait_ge(S[f"v_spread{g % 2}"], nth(f"v_spread{g % 2}", i, 64 * (g // 2)))
                act.activation(v_out(step, 0), pairs2(pV[0:98, 0:2 * C]), ACT.Copy,
                               scale=1.0 / WSC).then_inc(S["v_act"], 1)

            def direct(i, p):
                act.wait_ge(S["max_d"], nth("max_d", i, 2 * p + 1))
                if due("norm_p", i, p - 1):
                    act.wait_ge(S["norm_p"], nth("norm_p", i, p - 1))
                for h in range(DH):
                    t = slice(NT * h, NT * h + NT)
                    a = act.activation(prob[:, p % 2, t], pS[:, 0, t], ACT.Exp, bias=mx[:, p % 2, h:h + 1],
                                       scale=-1.0, accum_out=den[:, p % 2, h:h + 1])
                a.then_inc(S["direct_a"], 1)

            def exp(i, p):
                act.wait_ge(S["sub_d"], nth("sub_d", i, p + 1))
                act.activation(prob[:, p % 2, DC:], prob[:, p % 2, DC:], ACT.Exp, scale=-1.0).then_inc(S["exp_a"], 1)

            def turned_hi(i, p):
                act.wait_ge(S["t_pe"], nth("t_pe", i, p + 1))
                if due("o_pe", i, p - 1):
                    act.wait_ge(S["o_pe"], nth("o_pe", i, p - 1))
                act.activation(pT[0:98, p % 2, 0], turned(), ACT.Copy, scale=PSC).then_inc(S["t_act"], 1)

            def out_hi(i, k):
                act.wait_ge(S["o_pe"], nth("o_pe", i, 2 * k + 2))
                r = k // 2
                if k % 2 == 0:
                    if due("pj_pe", i, 2 * (r - 1)):
                        act.wait_ge(S["pj_pe"], nth("pj_pe", i, 2 * (r - 1)))
                t = slice(196 * (k % 2), 196 * (k % 2) + 196)
                act.activation(pairs2(om[:, r % 2, 0, t]), pO[:, :, 0, 0:98], ACT.Copy, scale=1.0 / PSC)
                act.activation(pairs2(ot[0:64, r % 2, t]), pO[0:64, :, 1, 0:98], ACT.Copy,
                               scale=1.0 / PSC).then_inc(S["o_act"], 1)

            def project_out(i, r, tail):
                act.wait_ge(S["pj_pe"], nth("pj_pe", i, 2 * r + tail + 1))
                if due("x1_p", i, 2 * r + tail - 1):
                    act.wait_ge(S["x1_p"], nth("x1_p", i, 2 * r + tail - 1))
                h = 64 * (r // 4)
                if tail:
                    act.activation(pjt[h:h + 64, 1, :], tail_bank(r)[0:64, 0:ROW], ACT.Identity,
                                   bias=bp[0:64, 1:2], scale=1.0 / WSC).then_inc(S["pj_act"], 1)
                else:
                    act.activation(pjt[:, 0, :], pV[:, 0:ROW], ACT.Identity, bias=bp[:, 0:1],
                                   scale=1.0 / WSC).then_inc(S["pj_act"], 1)

            def body(i, prev, att, nxt):
                for p in range(PAIRS):
                    v = before(v_step, p, prev, att, nxt)
                    if v:
                        v_hi(i + v[0], v[1])
                    for n, row, tail in before(proj_step, p, prev, att, nxt):
                        project_out(i + n, row, tail)
                    if att:
                        direct(i, p)
                    if p % 2 and (p >= 3 and att or p < 3 and prev):
                        out_hi(i if p >= 3 else i - 1, ((p - 3) % PAIRS) // 2)
                    b = blur_step(p, 12, prev)
                    if b is not None:
                        act.wait_ge(S["c1_pe"], nth("c1_pe", i - 1, b + 1))
                        if b >= 2:
                            act.wait_ge(S["c2_pe"], nth("c2_pe", i - 1, b - 1))
                        act.activation(z[:, b % 2, 0, :], pM[0:SY, 0:3 * SY], ACT.Copy,
                                       scale=1.0 / ASC).then_inc(S["z_act"], 1)
                    if att:
                        exp(i, p)
                    if p >= 1 and att or p < 1 and prev:
                        turned_hi(i if p >= 1 else i - 1, (p - 1) % PAIRS)
                    n = norm_step(p, att, nxt)
                    if n:
                        norm(i + n[0], n[1], n[2])
                    b = blur_step(p, 10, prev)
                    if b is not None:
                        act.wait_ge(S["xcf_p"], nth("xcf_p", i - 1, b + 1))
                        if b >= 2:
                            act.wait_ge(S["c1_pe"], nth("c1_pe", i - 1, b - 1))
                        act.copy(xc[:, b % 2, 0, :], xcf[0:SY, b % 2, :]).then_inc(S["xch_a"], 1)
                    q = qk_step(p, att, nxt)
                    if q:
                        qk_hi(i + q[0], q[1], q[2])

            bodies(act, body)

        @block.vector
        def _(dve):
            count = [0]

            def then(ins):
                count[0] += 1
                ins.then_inc(S["setup"], 1)
                dve.wait_ge(S["setup"], count[0])

            then(dve.memset(tabs[:, 1, :], 0.0))
            dve.wait_ge(S["const_in"], 13 * 16)
            ri = xm[:, 1, 0:NT * NT].bitcast(I32)
            then(dve.tensor_scalar(hot[0][:, 0:NT * NT], ri, const("iota")[:, 0:1], None, ALU.is_equal))
            then(dve.tensor_scalar(hot[1][:, 0:NT * NT], ri, const("iota")[:, 1:2], None, ALU.is_equal))
            then(dve.tensor_copy(tabh[:, 0, :, :], tabs))
            then(dve.tensor_tensor(tabh[:, 1, :, :], tabs, tabh[:, 0, :, :], ALU.subtract))
            assert count[0] == SET_HOT, count
            then(dve.memset(mhalf[:, :], -0.5))
            wf = xm[:, 0, 0:8 * C]
            then(dve.tensor_scalar(wf, wf, WSC, None, ALU.mult))
            then(dve.tensor_copy(wmh[:, :], wf[:, 0:4 * C]))
            then(dve.tensor_copy(wth[:, :], wf[:, 4 * C:8 * C]))
            then(dve.tensor_tensor(wml[:, :], wf[:, 0:4 * C], wmh[:, :], ALU.subtract))
            then(dve.tensor_tensor(wtl[:, :], wf[:, 4 * C:8 * C], wth[:, :], ALU.subtract))
            then(dve.memset(vv[:, :, :, :, :, :], 0.0))
            for b in (0, 1):
                then(dve.memset(qst[:, b, NHP * CHUNK:NHP * CHUNK + QPAD], 0.0))
            off, rnd, sub = (xt[0:SY, 0, 2 * POS * n:2 * POS * (n + 1)] for n in (0, 1, 2))
            then(dve.tensor_scalar(off, off, FAR, -FAR, ALU.min, ALU.max))
            then(dve.tensor_scalar(rnd, off, ROUND, None, ALU.add))
            then(dve.tensor_scalar(rnd, rnd, ROUND, None, ALU.subtract))
            then(dve.tensor_tensor(sub, off, rnd, ALU.subtract))
            u0 = const("u0", SY).rearrange("p (o y) -> p o y", o=1).to_broadcast([SY, 2 * POS, HW])
            then(dve.tensor_tensor(dist, u0, spread(rnd, HW), ALU.add))
            then(dve.tensor_tensor(gauss, dist, spread(sub, HW), ALU.add))
            then(dve.tensor_tensor(gauss, gauss, gauss, ALU.mult))
            tp = const("taps", SY).rearrange("p (o t) -> p o t", o=1).to_broadcast([SY, 2 * POS, TAPS])
            then(dve.tensor_tensor(tapv, tp, spread(sub, TAPS), ALU.add))
            then(dve.tensor_tensor(tapv, tapv, tapv, ALU.mult))
            assert count[0] == SET_GAUSS, count
            then(dve.tensor_tensor(dist, dist, dist, ALU.mult))
            then(dve.tensor_scalar(dist, dist, (TAPS // 2 + 0.5) ** 2, None, ALU.is_le))
            inside, upper = (xt[0:SY, 0, 2 * POS * n:2 * POS * (n + 1)] for n in (3, 4))
            then(dve.tensor_scalar(inside, rnd, const("ys", SY), -0.5, ALU.add, ALU.is_ge))
            then(dve.tensor_scalar(upper, rnd, const("ys", SY), HW - 0.5, ALU.add, ALU.is_le))
            then(dve.tensor_tensor(inside, inside, upper, ALU.mult))
            dve.wait_ge(S["setup_act"], 2)
            then(dve.tensor_reduce(upper, tapv, AX.X, ALU.add))
            then(dve.reciprocal(upper, upper))
            then(dve.scalar_tensor_tensor(out=inside, in0=upper, scalar=ASC, in1=inside, op0=ALU.mult, op1=ALU.mult))
            then(dve.tensor_tensor(gauss, gauss, dist, ALU.mult))
            then(dve.tensor_tensor(gauss, gauss, spread(inside, HW), ALU.mult))
            for s in (0, 1):
                v = slice(HW * s, HW * s + HW)
                m = const("smask", SY)[:, s:s + 1]
                then(dve.tensor_scalar(amat[:, 0, :, v], gauss, m, None, ALU.mult))
                then(dve.scalar_tensor_tensor(out=amat[:, 1, :, v], in0=gauss, scalar=m,
                                              in1=amat[:, 0, :, v], op0=ALU.mult, op1=ALU.subtract))
            then(dve.memset(biasT[:, :], 0.0))
            dve.wait_ge(S["setup_pe"], 1)
            bt = heads(biasT[:, :])
            for row, bank in ((0, pT_), (64, pS)):
                for half, j0, j1 in ((0, 0, 42), (1, 42, NT)):
                    src = hot_out(bank)[0:NT, half, 0:NH * (j1 - j0)].rearrange("p (j h) -> p h j", h=NH)
                    then(dve.tensor_copy(bt[row:row + NT, :, j0:j1], src))
            assert count[0] == SET_ALL, count

            def tail_lo(i, c, s):
                row = 2 * c + s % 2
                dve.wait_ge(S["xnh_a"], nth("xnh_a", i, 4 * c + s + 1))
                t = slice(ROW * (row % 4), ROW * (row % 4) + ROW)
                dve.tensor_tensor(xnt[64:128, t], xnf[0:64, s % 2, :], xnt[0:64, t],
                                  ALU.subtract).then_inc(S["xtl_d"], 1)

            def qk_lo(i, c, g):
                dve.wait_ge(S["qk_act"], nth("qk_act", i, 6 * c + g + 1))
                blk, t, ps = g // 2, slice(ROW * (g % 2), ROW * (g % 2) + ROW), pQ[:, 0:ROW]
                qs = -HD ** -0.5 / WSC

                def low(o, hi, rows, scale):
                    return dve.scalar_tensor_tensor(out=o, in0=ps[rows], scalar=scale, in1=hi,
                                                    op0=ALU.mult, op1=ALU.subtract)
                a, k = slice(0, 128), const("kmask")
                if blk == 0:
                    last = low(qks[:, 1, t], qks[:, 0, t], a, qs)
                elif blk == 1:
                    for odd in (0, 1):
                        last = low(qks[:, 4 + odd, t], qks[:, 2 + odd, t], a, k[:, odd:odd + 1])
                else:
                    low(mix[:, 2, t], mix[:, 0, t], a, const("tscale"))
                    a = slice(64, 128)
                    last = low(mix[a, 3, t], mix[a, 1, t], a, k[a, 1:2])
                last.then_inc(S["qk_dve"], 1)

            def v_lo(i, step):
                dve.wait_ge(S["v_act"], nth("v_act", i, step + 1))
                dve.scalar_tensor_tensor(out=v_out(step, 1), in0=pairs2(pV[0:98, 0:2 * C]), scalar=1.0 / WSC,
                                         in1=v_out(step, 0), op0=ALU.mult,
                                         op1=ALU.subtract).then_inc(S["v_dve"], 1)

            def maximum(i, p, bank):
                if bank == 0:
                    dve.wait_ge(S["s_pe"], nth("s_pe", i, p + 1))
                    dve.tensor_reduce(mx[:, p % 2, 0:DH], heads(pS[:, 0, 0:DC]), AX.X,
                                      ALU.min).then_inc(S["max_d"], 1)
                else:
                    dve.tensor_reduce(mx[:, p % 2, DH:NH], heads(pS[:, 1, 0:NH * NT - DC]), AX.X,
                                      ALU.min).then_inc(S["max_d"], 1)

            def subtract(i, p):
                dve.wait_ge(S["max_d"], nth("max_d", i, 2 * p + 2))
                if due("norm_p", i, p - 1):
                    dve.wait_ge(S["norm_p"], nth("norm_p", i, p - 1))
                dve.tensor_tensor(heads(prob[:, p % 2, DC:]), heads(pS[:, 1, 0:NH * NT - DC]),
                                  spread(mx[:, p % 2, DH:NH], NT), ALU.subtract).then_inc(S["sub_d"], 1)

            def denominators(i, p):
                dve.wait_ge(S["exp_a"], nth("exp_a", i, p + 1))
                dve.tensor_reduce(den[:, p % 2, DH:NH], heads(prob[:, p % 2, DC:]), AX.X,
                                  ALU.add).then_inc(S["sum_d"], 1)

            def inverse(i, p):
                dve.wait_ge(S["sum_d"], nth("sum_d", i, p + 1))
                dve.reciprocal(den[:, p % 2, :], den[:, p % 2, :]).then_inc(S["rden_d"], 1)

            def turned_lo(i, p):
                dve.wait_ge(S["t_act"], nth("t_act", i, p + 1))
                dve.scalar_tensor_tensor(out=pT[0:98, p % 2, 1], in0=turned(), scalar=PSC,
                                         in1=pT[0:98, p % 2, 0], op0=ALU.mult,
                                         op1=ALU.subtract).then_inc(S["t_dve"], 1)

            def out_lo(i, k):
                dve.wait_ge(S["o_act"], nth("o_act", i, k + 1))
                r, t = k // 2, slice(196 * (k % 2), 196 * (k % 2) + 196)
                dve.scalar_tensor_tensor(out=pairs2(om[:, r % 2, 1, t]), in0=pO[:, :, 0, 0:98], scalar=1.0 / PSC,
                                         in1=pairs2(om[:, r % 2, 0, t]), op0=ALU.mult, op1=ALU.subtract)
                dve.scalar_tensor_tensor(out=pairs2(ot[64:128, r % 2, t]), in0=pO[0:64, :, 1, 0:98],
                                         scalar=1.0 / PSC, in1=pairs2(ot[0:64, r % 2, t]), op0=ALU.mult,
                                         op1=ALU.subtract).then_inc(S["o_dve"], 1)

            def aggregate(n, i):
                name = f"gn{n + 1}_dve"
                dve.bn_aggr(gmv[n][:, 0, :], gst[n][:, 0:8, :]).then_inc(S[name], 1)
                dve.bn_aggr(gmv[n][:, 1, :], gst[n][:, 8:12, :]).then_inc(S[name], 1)

            def center(n, i, ps):
                name = f"gn{n + 1}_dve"
                dve.wait_ge(S[f"gn{n + 1}_pe"], nth(f"gn{n + 1}_pe", i, 1))
                dve.tensor_copy(gmean[n][:, :], ps[:, 0:2]).then_inc(S[name], 1)
                dve.wait_ge(S[name], nth(name, i, 3))
                dve.tensor_tensor(gd[n][:, :], gmv[n][:, :, 0], gmean[n][:, :], ALU.subtract).then_inc(S[name], 1)
                dve.wait_ge(S[name], nth(name, i, 4))
                dve.tensor_tensor(gd[n][:, :], gd[n][:, :], gd[n][:, :], ALU.mult).then_inc(S[name], 1)
                dve.wait_ge(S[name], nth(name, i, 5))
                dve.tensor_tensor(gv[n][:, :], gd[n][:, :], gmv[n][:, :, 1], ALU.add).then_inc(S[name], 1)

            def add_eps(n, i, ps):
                dve.wait_ge(S[f"gn{n + 1}_pe"], nth(f"gn{n + 1}_pe", i, 2))
                dve.tensor_scalar(gve[n][:, :], ps[:, 0:2], EPS, None, ALU.add).then_inc(S[f"gn{n + 1}_dve"], 1)

            def body(i, prev, att, nxt):
                for p in range(PAIRS):
                    rows = [(n, r) for n, on in ((0, att), (-1, prev)) for r in range(NWX)
                            if on and p == PPR * r + 8 + n * PAIRS]
                    for n, r in rows:
                        dve.wait_ge(S["x1_p"], nth("x1_p", i + n, 2 * r + 1))
                    if prev and p == 4:
                        dve.wait_ge(S["x1_p"], nth("x1_p", i - 1, 16))
                    if prev and p == 5:
                        dve.wait_ge(S["gn2_bn"], nth("gn2_bn", i - 1, 12))
                    if nxt and p == 8:
                        dve.wait_ge(S["x_in"], nth("x_in", i + 1, 64))
                    if nxt and p == 12:
                        dve.wait_ge(S["gn1_bn"], nth("gn1_bn", i + 1, 12))
                    if p >= 2 and att or p < 2 and prev:
                        turned_lo(i if p >= 2 else i - 1, (p - 2) % PAIRS)
                    if prev and p == 5:
                        aggregate(1, i - 1)
                    if nxt and p == 12:
                        aggregate(0, i + 1)
                    b = blur_step(p, 13, prev)
                    if b is not None:
                        dve.wait_ge(S["c2_pe"], nth("c2_pe", i - 1, b + 1))
                        y = xr[:, BC * HW * b:BC * HW * (b + 1)]
                        dve.scalar_tensor_tensor(out=y, in0=pM[0:SY, 0:3 * SY], scalar=1.0 / ASC, in1=y,
                                                 op0=ALU.mult, op1=ALU.add).then_inc(S["y_dve"], 1)
                    if att:
                        maximum(i, p, 0)
                    if att:
                        maximum(i, p, 1)
                    if att:
                        subtract(i, p)
                    m = norm_step(p - 1, att, nxt)
                    if m and m[2] >= 2:
                        tail_lo(i + m[0], m[1], m[2])
                    if prev and p == 10:
                        dve.wait_ge(S["gn2_pe"], nth("gn2_pe", i - 1, 3))
                        dve.tensor_copy(coef[:, :, :], pM[0:SY, 0:2 * CC].rearrange("p (a c) -> p a c", a=2)
                                        ).then_inc(S["gn2_dve"], 1)
                    v = before(v_step, p, prev, att, nxt)
                    if v:
                        v_lo(i + v[0], v[1])
                    if nxt and p == 13:
                        center(0, i + 1, pV)
                    if nxt and p == 17:
                        add_eps(0, i + 1, pV)
                        dve.tensor_scalar(gneg[:, :], gmean[0][:, :], -1.0, None, ALU.mult).then_inc(S["gn1_dve"], 1)
                    if prev and p == 7:
                        add_eps(1, i - 1, pM)
                    q = before(qk_step, p, prev, att, nxt)
                    if q:
                        qk_lo(i + q[0], q[1], q[2])
                    if p % 2 and (p >= 3 and att or p < 3 and prev):
                        out_lo(i if p >= 3 else i - 1, ((p - 3) % PAIRS) // 2)
                    if prev and p == 6:
                        center(1, i - 1, pM)
                    if att:
                        denominators(i, p)
                    b = blur_step(p, 12, prev)
                    if b is not None:
                        dve.wait_ge(S["z_act"], nth("z_act", i - 1, b + 1))
                        dve.scalar_tensor_tensor(out=z[:, b % 2, 1, :], in0=pM[0:SY, 0:3 * SY], scalar=1.0 / ASC,
                                                 in1=z[:, b % 2, 0, :], op0=ALU.mult,
                                                 op1=ALU.subtract).then_inc(S["z_dve"], 1)
                    if att:
                        inverse(i, p)
                    for n, r in rows:
                        dve.bn_stats(gst[1][:, r, :], xm[:, par(i + n), ROW * r:ROW * r + ROW]
                                     ).then_inc(S["gn2_bn"], 1)
                    if prev and p == 4:
                        for t in range(4):
                            dve.bn_stats(gst[1][:, 8 + t, :],
                                         xt[:, par(i - 1), ROW * t:ROW * t + ROW]).then_inc(S["gn2_bn"], 1)
                    if nxt and 8 <= p < 12:
                        for r in range(3 * (p - 8), 3 * (p - 8) + 3):
                            src = xm[:, par(i + 1), ROW * r:ROW * r + ROW] if r < 8 else \
                                xt[:, par(i + 1), ROW * (r - 8):ROW * (r - 7)]
                            dve.bn_stats(gst[0][:, r, :], src).then_inc(S["gn1_bn"], 1)
                    if prev and p == 8:
                        dve.wait_ge(S["gn2_pool"], nth("gn2_pool", i - 1, 1))
                        dve.scalar_tensor_tensor(out=gnb[:, :], in0=gmean[1][:, :], scalar=-1.0, in1=grs[1][:, :],
                                                 op0=ALU.mult, op1=ALU.mult).then_inc(S["gn2_dve"], 1)
                        dve.wait_ge(S["gn2_dve"], nth("gn2_dve", i - 1, 8))
                        if due("xcl_p", i - 1, 0):
                            dve.wait_ge(S["xcl_p"], nth("xcl_p", i - 1, 0))
                        for n, g in enumerate((grs[1], gnb)):
                            dve.tensor_scalar(cmain[:, n, :], const("sm"), g[:, 0:1], None,
                                              ALU.mult).then_inc(S["gn2_dve"], 1)
                            dve.tensor_scalar(ctail[:, n, :], const("sm", CT)[:, 0:CT // 2], g[0:64, 1:2], None,
                                              ALU.mult).then_inc(S["gn2_dve"], 1)

            bodies(dve, body)

        @block.gpsimd
        def _(pool):
            pool.wait_ge(S["setup"], SET_ALL)

            def norm_lo(i, c, s):
                row = 2 * c + s
                pool.wait_ge(S["xnh_a"], nth("xnh_a", i, 4 * c + s + 1))
                t = slice(ROW * (row % 4), ROW * (row % 4) + ROW)
                pool.tensor_tensor(xnl[:, t], xnf[:, s, :], xnh[:, t], ALU.subtract).then_inc(S["xnl_p"], 1)
                pool.wait_ge(S["xnl_p"], nth("xnl_p", i, 2 * c + s + 1))

            def add_residual(i, r, tail):
                pool.wait_ge(S["pj_act"], nth("pj_act", i, 2 * r + tail + 1))
                pool.wait_ge(S["xnh_a"], nth("xnh_a", i, 4 * (r // 2) + 4))
                if tail:
                    h, t = 64 * (r // 4), slice(ROW * (r % 4), ROW * (r % 4) + ROW)
                    v, a = windows(xt[h:h + 64, par(i), t]), wmajor(pjt[h:h + 64, 1, :])
                else:
                    v, a = windows(xm[:, par(i), ROW * r:ROW * r + ROW]), wmajor(pjt[:, 0, :])
                pool.tensor_tensor(v, v, a, ALU.add).then_inc(S["x1_p"], 1)
                pool.wait_ge(S["x1_p"], nth("x1_p", i, 2 * r + tail + 1))

            def body(i, prev, att, nxt):
                for p in range(PAIRS):
                    if nxt and p == 18:
                        pool.wait_ge(S["gn1_dve"], nth("gn1_dve", i + 1, 8))
                        if due("xnh_a", i, 16):
                            pool.wait_ge(S["xnh_a"], nth("xnh_a", i, 16))
                        pool.tensor_tensor(grs[0][:, :], gve[0][:, :], mhalf[:, :],
                                           ALU.pow).then_inc(S["gn1_pool"], 1)
                        pool.wait_ge(S["gn1_pool"], nth("gn1_pool", i + 1, 1))
                        pool.tensor_tensor(gbias[:, :], gneg[:, :], grs[0][:, :], ALU.mult).then_inc(S["gn1_pool"], 1)
                        pool.wait_ge(S["gn1_pool"], nth("gn1_pool", i + 1, 2))
                    b = blur_step(p, 11, prev)
                    if b is not None:
                        pool.wait_ge(S["xch_a"], nth("xch_a", i - 1, b + 1))
                        pool.tensor_tensor(xc[:, b % 2, 1, :], xcf[0:SY, b % 2, :], xc[:, b % 2, 0, :],
                                           ALU.subtract).then_inc(S["xcl_p"], 1)
                        pool.wait_ge(S["xcl_p"], nth("xcl_p", i - 1, b + 1))
                    b = blur_step(p, 10, prev)
                    if b is not None:
                        if b == 0:
                            pool.wait_ge(S["xr_in"], nth("xr_in", i - 1, 64))
                            pool.wait_ge(S["gn2_dve"], nth("gn2_dve", i - 1, 13))
                        cols = slice(BC * b, BC * b + BC)
                        v = xcf[0:SY, b % 2, :].rearrange("p (c x) -> p c x", x=HW)
                        src = xr[:, BC * HW * b:BC * HW * (b + 1)].rearrange("p (c x) -> p c x", x=HW)
                        pool.tensor_tensor(v, src, spread(coef[:, 0, cols], HW), ALU.mult).then_inc(S["xcm_p"], 1)
                        pool.wait_ge(S["xcm_p"], nth("xcm_p", i - 1, b + 1))
                        pool.tensor_tensor(v, v, spread(coef[:, 1, cols], HW), ALU.add).then_inc(S["xcf_p"], 1)
                        pool.wait_ge(S["xcf_p"], nth("xcf_p", i - 1, b + 1))
                    n = norm_step(p - 1, att, nxt)
                    if n and n[2] < 2:
                        norm_lo(i + n[0], n[1], n[2])
                    for n, row, tail in before(proj_step, p, prev, att, nxt):
                        add_residual(i + n, row, tail)
                    if prev and p == 8:
                        pool.wait_ge(S["gn2_dve"], nth("gn2_dve", i - 1, 7))
                        pool.tensor_tensor(grs[1][:, :], gve[1][:, :], mhalf[:, :],
                                           ALU.pow).then_inc(S["gn2_pool"], 1)
                        pool.wait_ge(S["gn2_pool"], nth("gn2_pool", i - 1, 1))
                    if att:
                        pool.wait_ge(S["rden_d"], nth("rden_d", i, p + 1))
                        if due("t_pe", i, p - 1):
                            pool.wait_ge(S["t_pe"], nth("t_pe", i, p - 1))
                        pool.tensor_tensor(heads(probn[:, p % 2, :]), heads(prob[:, p % 2, :]),
                                           spread(den[:, p % 2, :], NT), ALU.mult).then_inc(S["norm_p"], 1)
                        pool.wait_ge(S["norm_p"], nth("norm_p", i, p + 1))

            bodies(pool, body)


def kernel(x, L0_conv_w_qkv, L0_conv_w_proj, L0_conv_b_proj, L0_conv_bias_table, L0_conv_rel_index,
           L1_conv_offset):
    import concourse.bacc as bacc
    from concourse.bass_utils import run_bass_kernel_spmd as run

    x, wq, wp = (np.asarray(a) for a in (x, L0_conv_w_qkv, L0_conv_w_proj))
    q, k, v = wq[:C].T, wq[C:2 * C].T, wq[2 * C:].T
    v = v.reshape(C, NHP, 2, HD).transpose(0, 2, 3, 1).reshape(C, C)
    w = np.concatenate([q[:, :CM], k[:, :CM], q[:, CM:], k[:, CM:], v, wp.T], 1)
    cf, ch = constants()
    arrays = {"in_x": x, "in_w": np.ascontiguousarray(w),
              "in_b": np.asarray(L0_conv_b_proj).reshape(C, 1), "in_table": np.asarray(L0_conv_bias_table),
              "in_rel": np.asarray(L0_conv_rel_index), "in_offset": np.asarray(L1_conv_offset),
              "in_cf": cf, "in_ch": ch}
    nc = bacc.Bacc("TRN2", target_bir_lowering=False, num_devices=1)
    aps = [nc.dram_tensor(n, a.shape, mybir.dt.from_np(a.dtype), kind="ExternalInput").ap()
           for n, a in arrays.items()]
    scratch = nc.dram_tensor("x1_scratch", (C, TOK), F32, kind="Internal").ap()
    out = nc.dram_tensor("out_0", x.shape, F32, kind="ExternalOutput").ap()
    build(nc, *aps, scratch, out)
    r = run(nc, [arrays], core_ids=[0])
    return r.results[0]["out_0"]
```
